# Optimizing a Trainium2 kernel written in Bass

```python
import numpy as np
import jax
import jax.numpy as jnp

def _softmax(x, axis=-1):
    return jax.nn.softmax(x, axis=axis)

def _gelu(x):
    return jax.nn.gelu(x, approximate=True)

def _silu(x):
    return jax.nn.silu(x)

def _sigmoid(x):
    return jax.nn.sigmoid(x)

def _layernorm(x, axis=-1, eps=1e-05):
    m = jnp.mean(x, axis=axis, keepdims=True)
    v = jnp.var(x, axis=axis, keepdims=True)
    return (x - m) / jnp.sqrt(v + eps)

def _scatter_add(tgt, idx, src, axis=0):
    return tgt.at[idx].add(src)

def _segment_sum(src, seg, n):
    return jax.ops.segment_sum(src, seg, n)
kernel_name = 'mk_adaln_d1_jaxref_r8_eeecfd'

def setup_inputs(seed: int=0):
    np.random.seed(seed)
    _w = jnp.asarray

    def _L0_attn_setup():
        import jax, jax.numpy as jnp
        import numpy as np
        B, L, E, H = (2, 512, 128, 16)
        D = E // H
        CHUNK = 32

        def _linear_attention(x, W_qkv, W_out):
            Bz, Lz, Ez = x.shape
            scale = D ** (-0.5)
            qkv = x @ W_qkv.T
            qkv = qkv.reshape(Bz, Lz, 3, H, D).transpose(2, 0, 3, 1, 4)
            q, k, v = (qkv[0], qkv[1], qkv[2])
            q = (jax.nn.elu(q) + 1.0) * scale
            k = jax.nn.elu(k) + 1.0
            nc = Lz // CHUNK

            def to_chunks(t):
                return t.reshape(Bz, H, nc, CHUNK, D).transpose(2, 0, 1, 3, 4)
            qc, kc, vc = (to_chunks(q), to_chunks(k), to_chunks(v))
            causal = jnp.tril(jnp.ones((CHUNK, CHUNK), dtype=x.dtype))

            def step(carry, inp):
                S, Z = carry
                qi, ki, vi = inp
                attn = jnp.einsum('bhld,bhmd->bhlm', qi, ki) * causal
                num = jnp.einsum('bhlm,bhme->bhle', attn, vi) + jnp.einsum('bhld,bhde->bhle', qi, S)
                den = attn.sum(-1) + jnp.einsum('bhld,bhd->bhl', qi, Z)
                S = S + jnp.einsum('bhmd,bhme->bhde', ki, vi)
                Z = Z + ki.sum(axis=2)
                return ((S, Z), (num, den))
            S0 = jnp.zeros((Bz, H, D, D), dtype=x.dtype)
            Z0 = jnp.zeros((Bz, H, D), dtype=x.dtype)
            _, (num, den) = jax.lax.scan(step, (S0, Z0), (qc, kc, vc))
            num = num.transpose(1, 2, 0, 3, 4).reshape(Bz, H, Lz, D)
            den = den.transpose(1, 2, 0, 3).reshape(Bz, H, Lz)
            den = jnp.maximum(den, 1e-06)
            out = num / den[..., None]
            out = out.transpose(0, 2, 1, 3).reshape(Bz, Lz, Ez)
            return out @ W_out.T
        key = jax.random.key(seed)
        k1, k2, k3 = jax.random.split(key, 3)
        x = jax.random.normal(k1, (B, L, E), dtype=jnp.float32)
        W_qkv = jax.random.normal(k2, (3 * E, E), dtype=jnp.float32) * 0.02
        W_out = jax.random.normal(k3, (E, E), dtype=jnp.float32) * 0.02
        return {'x': x, 'W_qkv': W_qkv, 'W_out': W_out}
    _L0_attn_in = _L0_attn_setup()

    def _L0_ffn_setup():
        import jax, jax.numpy as jnp
        import numpy as np
        HIDDEN = 128
        NUM_EXPERTS = 8
        TOP_K = 2
        B, S = (2, 256)
        key = jax.random.key(seed)
        k1, k2, k3, k4, k5 = jax.random.split(key, 5)
        d, dff, E = (HIDDEN, 4 * HIDDEN, NUM_EXPERTS)
        x = jax.random.normal(k1, (B, S, d), dtype=jnp.float32)
        W1 = jax.random.normal(k2, (E, d, dff), dtype=jnp.float32) * (1.0 / np.sqrt(d))
        b1 = jax.random.normal(k3, (E, dff), dtype=jnp.float32) * 0.01
        W2 = jax.random.normal(k4, (E, dff, d), dtype=jnp.float32) * (1.0 / np.sqrt(dff))
        b2 = jax.random.normal(k5, (E, d), dtype=jnp.float32) * 0.01
        return {'x': x, 'W1': W1, 'b1': b1, 'W2': W2, 'b2': b2}
    _L0_ffn_in = _L0_ffn_setup()
    _L0_c = _w((lambda *s: np.random.randn(*s).astype(np.float32) * 0.05)(2, 128))
    _L0_wmod = _w((lambda *s: np.random.randn(*s).astype(np.float32) * 0.05)(128, 6 * 128) * 128 ** (-0.5))
    _d = {'L0_attn_x': _L0_attn_in['x'], 'L0_attn_W_qkv': _L0_attn_in['W_qkv'], 'L0_attn_W_out': _L0_attn_in['W_out'], 'L0_ffn_W1': _L0_ffn_in['W1'], 'L0_ffn_b1': _L0_ffn_in['b1'], 'L0_ffn_W2': _L0_ffn_in['W2'], 'L0_ffn_b2': _L0_ffn_in['b2'], 'L0_c': _L0_c, 'L0_wmod': _L0_wmod}
    _x0 = _d['L0_attn_x']
    _d['L0_attn_x'] = jax.random.normal(jax.random.fold_in(jax.random.key(seed), 1), (2, 1024, 128), dtype=_x0.dtype)
    del _x0
    return _d

def reference(L0_attn_x, L0_attn_W_qkv, L0_attn_W_out, L0_ffn_W1, L0_ffn_b1, L0_ffn_W2, L0_ffn_b2, L0_c, L0_wmod):

    def _L0_attn_ref(x, W_qkv, W_out):
        import jax, jax.numpy as jnp
        import numpy as np
        B, L, E, H = (2, 512, 128, 16)
        D = E // H
        CHUNK = 32

        def _linear_attention(x, W_qkv, W_out):
            Bz, Lz, Ez = x.shape
            scale = D ** (-0.5)
            qkv = x @ W_qkv.T
            qkv = qkv.reshape(Bz, Lz, 3, H, D).transpose(2, 0, 3, 1, 4)
            q, k, v = (qkv[0], qkv[1], qkv[2])
            q = (jax.nn.elu(q) + 1.0) * scale
            k = jax.nn.elu(k) + 1.0
            nc = Lz // CHUNK

            def to_chunks(t):
                return t.reshape(Bz, H, nc, CHUNK, D).transpose(2, 0, 1, 3, 4)
            qc, kc, vc = (to_chunks(q), to_chunks(k), to_chunks(v))
            causal = jnp.tril(jnp.ones((CHUNK, CHUNK), dtype=x.dtype))

            def step(carry, inp):
                S, Z = carry
                qi, ki, vi = inp
                attn = jnp.einsum('bhld,bhmd->bhlm', qi, ki) * causal
                num = jnp.einsum('bhlm,bhme->bhle', attn, vi) + jnp.einsum('bhld,bhde->bhle', qi, S)
                den = attn.sum(-1) + jnp.einsum('bhld,bhd->bhl', qi, Z)
                S = S + jnp.einsum('bhmd,bhme->bhde', ki, vi)
                Z = Z + ki.sum(axis=2)
                return ((S, Z), (num, den))
            S0 = jnp.zeros((Bz, H, D, D), dtype=x.dtype)
            Z0 = jnp.zeros((Bz, H, D), dtype=x.dtype)
            _, (num, den) = jax.lax.scan(step, (S0, Z0), (qc, kc, vc))
            num = num.transpose(1, 2, 0, 3, 4).reshape(Bz, H, Lz, D)
            den = den.transpose(1, 2, 0, 3).reshape(Bz, H, Lz)
            den = jnp.maximum(den, 1e-06)
            out = num / den[..., None]
            out = out.transpose(0, 2, 1, 3).reshape(Bz, Lz, Ez)
            return out @ W_out.T
        return _linear_attention(x, W_qkv, W_out)

    def _L0_ffn_ref(x, W1, b1, W2, b2):
        import jax, jax.numpy as jnp
        import numpy as np
        HIDDEN = 128
        NUM_EXPERTS = 8
        TOP_K = 2
        B, S = (2, 256)
        Bm, Sm, d = x.shape
        E = W1.shape[0]
        x_flat = x.reshape(-1, d)
        h = jnp.mod(x_flat[:, :TOP_K].sum(axis=1).astype(jnp.int32), E)
        sel = jnp.stack([h, jnp.mod(h + 1, E)], axis=1)

        def step(acc, params):
            e, W1e, b1e, W2e, b2e = params
            w = jnp.any(sel == e, axis=1).astype(x.dtype) / TOP_K
            y = jnp.maximum(x_flat @ W1e + b1e, 0.0) @ W2e + b2e
            return (acc + w[:, None] * y, None)
        init = jnp.zeros_like(x_flat)
        out_flat, _ = jax.lax.scan(step, init, (jnp.arange(E), W1, b1, W2, b2))
        return out_flat.reshape(Bm, Sm, d)
    x = L0_attn_x
    mod = (_silu(L0_c) @ L0_wmod).reshape(L0_c.shape[0], 6, 1, -1)
    sa, ca, ga, sb, cb, gb = (mod[:, 0], mod[:, 1], mod[:, 2], mod[:, 3], mod[:, 4], mod[:, 5])
    ga = (2 * (ga >= 0) - 1) * jnp.maximum(jnp.abs(ga), 0.25)
    gb = (2 * (gb >= 0) - 1) * jnp.maximum(jnp.abs(gb), 0.25)
    h = _layernorm(x, axis=-1) * (1 + ca) + sa
    x = x + ga * _L0_attn_ref(h, L0_attn_W_qkv, L0_attn_W_out)
    h = _layernorm(x, axis=-1) * (1 + cb) + sb
    x = x + gb * _L0_ffn_ref(h, L0_ffn_W1, L0_ffn_b1, L0_ffn_W2, L0_ffn_b2)
    return x

_drawn_inputs = setup_inputs


def setup_inputs(seed=0):
    import zlib

    import numpy as np

    out = dict(_drawn_inputs(seed))
    spreads = {}
    factors = {'L0_attn_W_qkv': 8.0, 'L0_attn_W_out': 8.0, 'L0_ffn_b1': 45.216, 'L0_ffn_b2': 32.261}
    for name, (base, spread) in spreads.items():
        noise = np.random.default_rng([zlib.crc32(name.encode()), seed]).standard_normal(out[name].shape)
        drawn = base * np.exp(spread * noise) if base else spread * noise
        out[name] = jnp.asarray(drawn.astype(out[name].dtype))
    for name, factor in factors.items():
        out[name] = (out[name] * factor).astype(out[name].dtype)
    return out
```

```python
from contextlib import ExitStack

import concourse.bass as bass
from concourse import mybir

F32 = mybir.dt.float32
F16 = mybir.dt.float16
I32 = mybir.dt.int32
ALU = mybir.AluOpType
ACT = mybir.ActivationFunctionType
AX = mybir.AxisListType

P = 128
B, L, E = 2, 1024, 128
HEADS = 16
D = E // HEADS
CHUNK = 32
HALF = 4
HALVES = L // (P * HALF)
STEPS = B * HALVES
TILES = B * L // P
CPT = P // CHUNK
CPH = HALF * CPT
HG = P // CHUNK
GROUPS = HEADS // HG
GW = HG * D + HG
NUM = HG * D
OW = GROUPS * GW
EXPERTS = 8
FF = 512
FC = FF // P
SLOTS = TILES + EXPERTS - 1
PLACES = TILES
NO_PLACE = EXPERTS * PLACES
LN_EPS = 1e-5
SCALE = float(D) ** -0.5
RSQRT_SEED = float(0x5F3759DF)
W = HALF * P


def build(nc, x_d, wqkv_d, wout_d, w1_d, b1_d, w2_d, b2_d, c_d, wmod_d, out_d):
    rows_d = nc.dram_tensor("rows_x1_h2", (B * L, 2 * E), F32, kind="Internal").ap()
    with ExitStack() as ctx:
        def sb(name, shape, dtype=F32):
            return ctx.enter_context(nc.sbuf_tensor(name, [P, *shape], dtype))

        def sem(name):
            return ctx.enter_context(nc.semaphore(name))

        ps = ctx.enter_context(nc.psum_tensor("ps", [P, 8, 512], F32))

        x_all = sb("x_all", [TILES, E])
        wqkv = sb("wqkv", [3, E])
        wout = sb("wout", [E])
        w_t = sb("w_t", [3 * E])
        wo_t = sb("wo_t", [E])
        wo_g = sb("wo_g", [B, E])
        wmod = sb("wmod", [6 * E])
        c_rows = sb("c_rows", [P])
        c_t = sb("c_t", [B])
        silu = sb("silu", [B])
        silu_tmp = sb("silu_tmp", [B])
        silu_bc = sb("silu_bc", [B, P])
        col_sa = sb("col_sa", [B])
        col_ca1 = sb("col_ca1", [B])
        row_mod = sb("row_mod", [B, 4, E])
        gate_abs = sb("gate_abs", [B, 2, E])
        gate_sgn = sb("gate_sgn", [B, 2, E])
        gates = sb("gates", [B, 2, E])
        row_cb1 = sb("row_cb1", [B, E])
        w1 = sb("w1", [EXPERTS + 1, FF])
        w2 = sb("w2", [EXPERTS + 1, FC, E])
        b1_rows = sb("b1_rows", [P])
        b1 = sb("b1", [(EXPERTS + 1) * FC])
        b2 = sb("b2", [EXPERTS + 1, E])
        b2_pair = sb("b2_pair", [EXPERTS, E])

        ident = sb("ident", [P])
        before = sb("before", [P], F16)
        ones = sb("ones", [P], F16)
        causal = sb("causal", [CHUNK])
        iota_row = sb("iota_row", [P])
        part_i = sb("part_i", [1], I32)
        part_f = sb("part_f", [1])
        part_far = sb("part_far", [1])
        part_i2 = sb("part_i2", [3], I32)
        part_f2 = sb("part_f2", [3])
        token1 = sb("token1", [TILES])
        col_head = sb("col_head", [GROUPS, GW])
        state_mask = sb("state_mask", [OW])
        head_mask = sb("head_mask", [HG])
        den_mask = sb("den_mask", [HG])

        def two(name, shape, dtype=F32):
            return [sb(f"{name}{h}", shape, dtype) for h in range(2)]

        def one(name, shape, dtype=F32):
            return [sb(name, shape, dtype)] * 2

        stats = sb("stats", [HALF, 6])
        mean_var = sb("mean_var", [HALF, 2])
        var = sb("var", [HALF])
        rs_a = sb("rs_a", [HALF])
        rs_b = sb("rs_b", [HALF])
        rstd = sb("rstd", [HALF])
        xn = two("xn", [HALF, E])
        h_t = one("h_t", [W])
        e_q = one("e_q", [W])
        e_k = one("e_k", [W])
        e_kt = one("e_kt", [HALF, P])
        q_t = one("q_t", [W])
        k_t = one("k_t", [W])
        q_hi = one("q_hi", [W], F16)
        q_lo = one("q_lo", [W], F16)
        k_hi = one("k_hi", [W], F16)
        k_lo = one("k_lo", [W], F16)
        kx_hi = one("kx_hi", [CPH, HG, CHUNK], F16)
        kx_lo = one("kx_lo", [CPH, HG, CHUNK], F16)
        k_tok = one("k_tok", [HALF, P])
        v_tok = one("v_tok", [HALF, GROUPS, GW])
        v_t = one("v_t", [W])
        vx_t = one("vx_t", [CPH, HG, CHUNK])
        vx = one("vx", [CPH, GROUPS, GW])
        attn = one("attn", [GROUPS, CPH, CHUNK])
        part = one("part", [HALF, CPT, OW])
        state = two("state", [HALF + 1, OW])
        den = two("den", [HEADS])
        rden = two("rden", [HEADS])
        heads_out = one("heads_out", [HALF, E])
        a_t = one("a_t", [W])
        rows = sb("rows", [TILES, 2, E])
        rt_s = sb("rt_s", [HALF])
        rt_t = sb("rt_t", [HALF])
        rt_i = sb("rt_i", [HALF], I32)
        rt_f = sb("rt_f", [HALF])
        rt_m = sb("rt_m", [HALF])
        rt_g = sb("rt_g", [HALF])
        rt_r = sb("rt_r", [HALF])
        rt_k = sb("rt_k", [HALF])
        rt_i2 = sb("rt_i2", [HALF], I32)
        rt_i3 = sb("rt_i3", [HALF], I32)
        onehot = sb("onehot", [HALF, EXPERTS], F16)
        earlier = sb("earlier", [HALF + 1, EXPERTS], F16)
        rank8 = sb("rank8", [HALF, EXPERTS])
        oh_place = sb("oh_place", [HALF, P], F16)
        oh_token = sb("oh_token", [HALF, P], F16)
        table = sb("table", [P])
        table16 = sb("table16", [P], F16)
        total = sb("total", [EXPERTS])
        tot_i = sb("tot_i", [EXPERTS], I32)
        tiles_of = sb("tiles_of", [EXPERTS])
        ends = sb("ends", [EXPERTS])
        passed = sb("passed", [SLOTS, EXPERTS])
        weighed = sb("weighed", [SLOTS, EXPERTS])
        slot_g = sb("slot_g", [SLOTS])
        slot_b = sb("slot_b", [SLOTS])
        slot_c = sb("slot_c", [SLOTS])
        slot_gi = sb("slot_gi", [SLOTS], I32)
        slot_gm = sb("slot_gm", [SLOTS], I32)
        pick = sb("pick", [SLOTS], F16)
        tok_f = sb("tok_f", [SLOTS])
        tok_e = sb("tok_e", [SLOTS])
        src_f = sb("src_f", [SLOTS])
        src_i = sb("src_i", [SLOTS], I32)
        dst_f = sb("dst_f", [SLOTS])
        dst_i = sb("dst_i", [SLOTS], I32)
        second = sb("second", [SLOTS])
        first = sb("first", [SLOTS])
        got = sb("got", [SLOTS, 2, E])
        h_row = sb("h_row", [E])
        h_col = sb("h_col", [P])
        free = attn[0][:, :, :, :].rearrange("p g c l -> p (g c l)")
        w1_now = free[:, 0:2 * FF].rearrange("p (x f) -> p x f", x=2)
        hid = free[:, 2 * FF:4 * FF].rearrange("p (x c t) -> p x c t", x=2, c=FC)
        y_b = sb("y_b", [E])
        gate_a = sb("gate_a", [E])
        gate_b = sb("gate_b", [E])
        y_g = sb("y_g", [E])
        done = got[:, :, 0, :]

        in_small = sem("in_small")
        in_x = sem("in_x")
        in_w1 = sem("in_w1")
        in_w2 = sem("in_w2")
        in_b2 = sem("in_b2")
        const = sem("const")
        consts = sem("consts")
        setup_pe = sem("setup_pe")
        setup_act = sem("setup_act")
        setup_dve = sem("setup_dve")
        pe_xT = sem("pe_xT")
        pe_q = sem("pe_q")
        pe_k = sem("pe_k")
        pe_vT = sem("pe_vT")
        pe_kv = sem("pe_kv")
        pe_vx = sem("pe_vx")
        pe_qk = sem("pe_qk")
        pe_ds = sem("pe_ds")
        pe_o = sem("pe_o")
        pe_aT = sem("pe_aT")
        pe_y = sem("pe_y")
        pe_rank = sem("pe_rank")
        pe_perm = sem("pe_perm")
        act_h = sem("act_h")
        act_eq = sem("act_eq")
        act_ek = sem("act_ek")
        act_vT = sem("act_vT")
        act_ekt = sem("act_ekt")
        act_vt = sem("act_vt")
        act_qhi = sem("act_qhi")
        act_khi = sem("act_khi")
        act_vx = sem("act_vx")
        act_aT = sem("act_aT")
        pool_eq = sem("pool_eq")
        pool_ek = sem("pool_ek")
        pool_vTx = sem("pool_vTx")
        pool_ekt = sem("pool_ekt")
        pool_kx = sem("pool_kx")
        pool_h2 = sem("pool_h2")
        dve_xn = sem("dve_xn")
        dve_q = sem("dve_q")
        dve_k = sem("dve_k")
        dve_kt = sem("dve_kt")
        dve_qlo = sem("dve_qlo")
        dve_klo = sem("dve_klo")
        dve_kx = sem("dve_kx")
        dve_at = sem("dve_at")
        dve_sm = sem("dve_sm")
        dve_st = sem("dve_st")
        dve_ao = sem("dve_ao")
        dve_x1 = sem("dve_x1")
        dve_xn2 = sem("dve_xn2")
        dve_oh = sem("dve_oh")
        dve_v = sem("dve_v")
        dve_perm = sem("dve_perm")
        dve_run = sem("dve_run")
        pe_total = sem("pe_total")
        dve_pick = sem("dve_pick")
        pe_slots = sem("pe_slots")
        dve_slots = sem("dve_slots")
        rows_out = sem("rows_out")
        gathered = sem("gathered")
        act_row = sem("act_row")
        pe_hT = sem("pe_hT")
        act_hT = sem("act_hT")
        pe_w1 = sem("pe_w1")
        act_hid = sem("act_hid")
        dve_hid = sem("dve_hid")
        pe_y2 = sem("pe_y2")
        dve_w1 = sem("dve_w1")
        dve_done = sem("dve_done")
        scattered = sem("scattered")
        b2_ready = sem("b2_ready")
        turns = sem("turns")

        def each(b, h, per_half, k):
            return b * (HALVES * per_half) + (h * per_half + k)

        def wait_alone(eng, semaphore, value):
            eng.wait_ge(semaphore, value)
            eng.sem_inc(turns, 1)

        block = ctx.enter_context(nc.Block())

        @block.sync
        def _(sp):
            with nc.allow_non_contiguous_dma(reason="rows of experts"):
                sp.dma_start(c_rows[0:B, :], c_d).then_inc(in_small, 16)
                sp.dma_start(x_all[:, 0:HALF, :], x_d[0:W, :].rearrange("(t p) e -> p t e", p=P)).then_inc(in_x, 16)
                sp.dma_start(wqkv[:, :, :], wqkv_d.rearrange("(g o) e -> o g e", o=P)).then_inc(in_small, 16)
                sp.dma_start(wmod[:, :], wmod_d).then_inc(in_small, 16)
                sp.dma_start(wout[:, :], wout_d).then_inc(in_small, 16)
                sp.dma_start(b1_rows[0:EXPERTS * FC, :], b1_d.rearrange("e (c p) -> (e c) p", p=P)).then_inc(in_small, 16)
                sp.dma_start(x_all[:, HALF:, :], x_d[W:, :].rearrange("(t p) e -> p t e", p=P)).then_inc(in_x, 16)
                sp.dma_start(b2[:, 0:EXPERTS, :], b2_d.rearrange("e d -> (e d)").partition_broadcast(P)
                             .rearrange("p (e d) -> p e d", d=E)).then_inc(in_b2, 16)
                sp.dma_start(b2[:, EXPERTS, :], b2_d[0, :].partition_broadcast(P)).then_inc(in_b2, 16)
                w1_v = w1_d.rearrange("e d f -> d e f")
                w2_v = w2_d.rearrange("e (c p) d -> p e c d", p=P)
                for e in range(EXPERTS):
                    sp.dma_start(w1[:, e, :], w1_v[:, e, :]).then_inc(in_w1, 16)
                    sp.dma_start(w2[:, e, :, :], w2_v[:, e, :, :]).then_inc(in_w2, 16)
                sp.dma_start(w1[:, EXPERTS, :], w1_v[:, 0, :]).then_inc(in_w1, 16)
                sp.dma_start(w2[:, EXPERTS, :, :], w2_v[:, 0, :, :]).then_inc(in_w2, 16)
                for u in range(STEPS):
                    sp.wait_ge(pool_h2, u + 1)
                    sp.dma_start(rows_d[u * W:(u + 1) * W, :].rearrange("(t p) c -> p t c", p=P),
                                 rows[:, u * HALF:(u + 1) * HALF, :, :].rearrange("p t a e -> p t (a e)")
                                 ).then_inc(rows_out, 16)
                sp.wait_ge(rows_out, 16 * STEPS)

        @block.gpsimd
        def _(pool):
            g = nc.gpsimd
            g.memset(ident[:, :], 0.0)
            g.memset(before[:, :], 1.0)
            g.memset(ones[:, :], 1.0)
            g.memset(causal[:, :], SCALE)
            imprecise = dict(allow_small_or_imprecise_dtypes=True)
            g.iota(iota_row[:, :], pattern=[[1, P]], base=0, channel_multiplier=0, **imprecise)
            g.iota(part_i[:, :], pattern=[[1, 1]], base=0, channel_multiplier=1)
            g.iota(part_f[:, :], pattern=[[1, 1]], base=0, channel_multiplier=1, **imprecise)
            g.iota(token1[:, :], pattern=[[P, TILES]], base=1, channel_multiplier=1, **imprecise)
            g.iota(col_head[:, :, 0:NUM].rearrange("p g (h d) -> p g h d", d=D),
                   pattern=[[HG, GROUPS], [1, HG], [0, D]], base=0, channel_multiplier=0, **imprecise)
            g.iota(col_head[:, :, NUM:GW], pattern=[[HG, GROUPS], [1, HG]], base=0, channel_multiplier=0,
                   **imprecise)
            pool.drain()
            g.affine_select(out=ident[:, :], in_=ident[:, :], compare_op=ALU.not_equal, fill=1.0, base=0,
                            pattern=[[-1, P]], channel_multiplier=1)
            g.affine_select(out=before[:, :], in_=before[:, :], compare_op=ALU.is_gt, fill=0.0, base=0,
                            pattern=[[1, P]], channel_multiplier=-1)
            for k in range(HG):
                pool.drain()
                rows_k = causal[k * CHUNK:(k + 1) * CHUNK, :]
                g.affine_select(out=rows_k, in_=rows_k, compare_op=ALU.is_ge, fill=0.0, base=0,
                                pattern=[[1, CHUNK]], channel_multiplier=-1)
            pool.drain()
            g.memset(state[0][:, 0, :], 0.0).then_inc(const, 1)
            pool.wait_ge(in_b2, 32)
            g.tensor_tensor(b2_pair[:, :, :], b2[:, 0:EXPERTS, :], b2[:, 1:EXPERTS + 1, :], ALU.add).then_inc(b2_ready, 1)
            pool.wait_ge(consts, 1)

            with pool.Fori(0, B) as b:
                for h in range(HALVES):
                    def min_one(dst):
                        return g.tensor_scalar(dst, dst, 1.0, None, ALU.min)
                    wait_alone(pool, act_eq, each(b, h, 1, 1))
                    min_one(e_q[h][:, :]).then_inc(pool_eq, 1)
                    wait_alone(pool, act_ek, each(b, h, 1, 1))
                    min_one(e_k[h][:, :]).then_inc(pool_ek, 1)
                    for n in range(2):
                        wait_alone(pool, act_ekt, each(b, h, 2, n + 1))
                        min_one(e_kt[h][:, 2 * n:2 * n + 2, :]).then_inc(pool_ekt, 1)
                    wait_alone(pool, act_vT, each(b, h, 1, 1))
                    for k in range(HG):
                        last = g.tensor_scalar(vx_t[h][:, :, k, :], v_t[h][:, :].rearrange("p (c m) -> p c m", m=CHUNK),
                                               head_mask[:, k:k + 1], None, ALU.mult)
                    last.then_inc(pool_vTx, 1)
                    wait_alone(pool, dve_klo, each(b, h, 1, 1))
                    for k in range(HG):
                        last = g.tensor_scalar(kx_lo[h][:, :, k, :], k_lo[h][:, :].rearrange("p (c m) -> p c m", m=CHUNK),
                                               head_mask[:, k:k + 1], None, ALU.mult)
                    last.then_inc(pool_kx, 1)
                    wait_alone(pool, dve_xn2, each(b, h, 1, 1))
                    h2 = rows[:, bass.ds((b * HALVES + h) * HALF, HALF), 1, :]
                    g.tensor_tensor(xn[h][:, :, :], xn[h][:, :, :],
                                    row_cb1[:, bass.ds(b, 1), :].broadcast_to([P, HALF, E]), ALU.mult)
                    pool.drain()
                    g.tensor_tensor(h2, xn[h][:, :, :],
                                    row_mod[:, bass.ds(b, 1), 1, :].broadcast_to([P, HALF, E]),
                                    ALU.add).then_inc(pool_h2, 1)

            pool.wait_ge(rows_out, 16 * STEPS)
            pool.wait_ge(dve_slots, 1)

            def gather(n):
                g.indirect_dma_start(out=got[:, n, :, :].rearrange("p a e -> p (a e)"), out_offset=None,
                                     in_=rows_d, in_offset=bass.IndirectOffsetOnAxis(ap=src_i[:, n:n + 1], axis=0)
                                     ).then_inc(gathered, 16)

            ahead = 3
            for n in range(ahead):
                if n:
                    pool.wait_ge(gathered, 16 * n)
                gather(n)
            for n in range(SLOTS):
                if n + ahead < SLOTS:
                    pool.wait_ge(gathered, 16 * (n + ahead))
                    gather(n + ahead)
                pool.wait_ge(dve_done, n + 1)
                g.indirect_dma_start(out=out_d, out_offset=bass.IndirectOffsetOnAxis(ap=dst_i[:, n:n + 1], axis=0),
                                     in_=done[:, n, :], in_offset=None, bounds_check=B * L - 1, oob_is_err=False
                                     ).then_inc(scattered, 16)
            pool.wait_ge(scattered, 16 * SLOTS)

        @block.scalar
        def _(act):
            a = nc.scalar
            act.wait_ge(setup_pe, 1)
            a.activation(c_t[:, :], ps[:, 0, 0:B], ACT.Copy)
            a.activation(w_t[:, :], ps[:, 1, 0:3 * E], ACT.Copy)
            a.activation(wo_t[:, :], ps[:, 2, 0:E], ACT.Copy)
            a.activation(b1[:, 0:EXPERTS * FC], ps[:, 3, 0:EXPERTS * FC], ACT.Copy)
            a.activation(b1[:, EXPERTS * FC:], ps[:, 3, 0:FC], ACT.Copy)
            act.drain()
            a.activation(silu_tmp[:, :], c_t[:, :], ACT.Exp, scale=-1.0).then_inc(setup_act, 1)
            act.wait_ge(consts, 1)

            with act.Fori(0, B) as b:
                for h in range(HALVES):
                    wait_alone(act, pe_xT, each(b, h, 1, 1))
                    a.activation(h_t[h][:, :], ps[:, 7, :], ACT.Identity, scale=col_ca1[:, bass.ds(b, 1)],
                                 bias=col_sa[:, bass.ds(b, 1)]).then_inc(act_h, 1)
                    act.wait_ge(pe_q, each(b, h, 1, 1))
                    a.activation(e_q[h][:, :], ps[:, 0, :], ACT.Exp).then_inc(act_eq, 1)
                    act.wait_ge(pe_k, each(b, h, 1, 1))
                    a.activation(e_k[h][:, :], ps[:, 1, :], ACT.Exp).then_inc(act_ek, 1)
                    act.wait_ge(pe_vT, each(b, h, 1, 1))
                    a.activation(v_t[h][:, :], ps[:, 4, :], ACT.Copy).then_inc(act_vT, 1)
                    for n in range(2):
                        kv = ps[:, 2 + n, :].rearrange("p (t c) -> p t c", t=2)
                        act.wait_ge(pe_kv, each(b, h, 2, n + 1))
                        a.activation(e_kt[h][:, 2 * n:2 * n + 2, :], kv[:, :, 0:P], ACT.Exp).then_inc(act_ekt, 1)
                        for t in range(2):
                            last = a.activation(v_tok[h][:, 2 * n + t, :, 0:NUM],
                                                kv[:, t, P:].rearrange("p (g c) -> p g c", g=GROUPS), ACT.Copy)
                        last.then_inc(act_vt, 1)
                    act.wait_ge(dve_q, each(b, h, 1, 1))
                    a.activation(q_hi[h][:, :], q_t[h][:, :], ACT.Copy).then_inc(act_qhi, 1)
                    act.wait_ge(dve_k, each(b, h, 1, 1))
                    a.activation(k_hi[h][:, :], k_t[h][:, :], ACT.Copy).then_inc(act_khi, 1)
                    for f in range(CPH // 4):
                        act.wait_ge(pe_vx, each(b, h, CPH // 4, f + 1))
                        a.activation(vx[h][:, 4 * f:4 * f + 4, :, 0:NUM].rearrange("p c g n -> p (c g) n"),
                                     ps[:, 6 + f % 2, :].rearrange("p (c n) -> p c n", n=NUM),
                                     ACT.Copy).then_inc(act_vx, 1)
                    act.wait_ge(pe_aT, each(b, h, 1, 1))
                    a.activation(a_t[h][:, :], ps[:, 7, :], ACT.Copy).then_inc(act_aT, 1)

            act.wait_ge(dve_slots, 1)
            with act.Fori(0, SLOTS) as n:
                expert = act.value_load(slot_gm[0:1, bass.ds(n, 1)], min_val=0, max_val=EXPERTS - 1)
                wait_alone(act, gathered, n * 16 + 16)
                a.activation(h_row[:, :], got[:, bass.ds(n, 1), 1, :], ACT.Copy).then_inc(act_row, 1)
                act.wait_ge(pe_hT, n + 1)
                a.activation(h_col[:, :], ps[:, 4, 0:P], ACT.Copy).then_inc(act_hT, 1)
                wait_alone(act, pe_w1, n * 2 + 1)
                for c in range(FC):
                    last = a.activation(hid[:, 0, c, :], ps[:, 0, c * P:(c + 1) * P], ACT.Relu,
                                        bias=b1[:, bass.ds(expert * FC + c, 1)])
                last.then_inc(act_hid, 1)

        @block.vector
        def _(dve):
            v = nc.vector
            order = dve.drain

            v.memset(table[:, :], 0.0)
            v.memset(v_tok[0][:, :, :, NUM:GW], 1.0)
            v.memset(earlier[:, 0, :], 0.0)
            dve.wait_ge(const, 1)
            v.tensor_scalar(part_i2[:, 0:1], part_i[:, :], 3, None, ALU.logical_shift_right)
            v.tensor_scalar(part_i2[:, 1:2], part_i[:, :], 3, HG - 1, ALU.logical_shift_right, ALU.bitwise_and)
            v.tensor_scalar(part_i2[:, 2:3], part_i[:, :], 5, None, ALU.logical_shift_right)
            order()
            v.tensor_copy(part_f2[:, :], part_i2[:, :])
            v.tensor_scalar(part_far[:, :], part_f[:, :], float(2 * B * L), None, ALU.add)
            order()
            v.tensor_scalar(head_mask[:, :], iota_row[:, 0:HG], part_f2[:, 1:2], None, ALU.is_equal)
            v.tensor_scalar(den_mask[:, :], iota_row[:, 0:HG], part_f2[:, 2:3], None, ALU.is_equal)
            v.tensor_scalar(state_mask[:, :], col_head[:, :, :].rearrange("p g c -> p (g c)"), part_f2[:, 0:1],
                            SCALE, ALU.is_equal, ALU.mult)
            order()
            v.tensor_copy(vx[0][:, :, :, NUM:GW].rearrange("p c g n -> p (c g) n"),
                          den_mask[:, :].unsqueeze(1).broadcast_to([P, CPH * GROUPS, HG]))
            dve.wait_ge(setup_act, 1)
            v.tensor_scalar(silu_tmp[:, :], silu_tmp[:, :], 1.0, None, ALU.add)
            order()
            v.reciprocal(silu[:, :], silu_tmp[:, :])
            order()
            v.tensor_tensor(silu[:, :], silu[:, :], c_t[:, :], ALU.mult)
            order()
            v.tensor_copy(silu_bc[:, :, :], silu[:, :].unsqueeze(2).broadcast_to([P, B, P])).then_inc(setup_dve, 1)
            dve.wait_ge(setup_pe, 2)
            v.tensor_copy(col_sa[:, :], ps[:, 4, 0:B])
            v.tensor_scalar(col_ca1[:, :], ps[:, 4, B:2 * B], 1.0, None, ALU.add)
            v.tensor_copy(row_mod[:, :, :, :].rearrange("p b m e -> p b (m e)"), ps[:, 5:7, :])
            order()
            v.tensor_scalar(row_cb1[:, :, :], row_mod[:, :, 2, :], 1.0, None, ALU.add)
            gate_raw = row_mod[:, :, 0:4:3, :]
            for b in range(B):
                v.scalar_tensor_tensor(gate_abs[:, b, :, :], gate_raw[:, b, :, :], -1.0, gate_raw[:, b, :, :],
                                       ALU.mult, ALU.max)
                v.tensor_scalar(gate_sgn[:, b, :, :], gate_raw[:, b, :, :], 0.0, 2.0, ALU.is_ge, ALU.mult)
            order()
            v.tensor_scalar(gate_abs[:, :, :, :], gate_abs[:, :, :, :], 0.25, None, ALU.max)
            v.tensor_scalar(gate_sgn[:, :, :, :], gate_sgn[:, :, :, :], -1.0, None, ALU.add)
            order()
            v.tensor_tensor(gates[:, :, :, :], gate_abs[:, :, :, :], gate_sgn[:, :, :, :], ALU.mult)
            order()
            v.tensor_scalar(gates[:, :, 1, :], gates[:, :, 1, :], 0.5, None, ALU.mult)
            v.tensor_tensor(wo_g[:, :, :], gates[:, :, 0, :], wo_t[:, :].unsqueeze(1).broadcast_to([P, B, E]), ALU.mult)
            order()
            v.memset(den[0][:, :], 0.0).then_inc(consts, 1)
            order()
            dve.wait_ge(in_x, 32)

            def norm(src, dst):
                for j in range(HALF):
                    v.bn_stats(out=stats[:, j, :], in_=src(j))
                order()
                for j in range(HALF):
                    v.bn_aggr(out=mean_var[:, j, :], in_=stats[:, j, :])
                order()
                v.tensor_scalar(var[:, :], mean_var[:, :, 1], LN_EPS, None, ALU.add)
                order()
                v.tensor_scalar(rstd[:, :].bitcast(I32), var[:, :].bitcast(I32), -0.5, RSQRT_SEED, ALU.mult, ALU.add)
                order()
                for _ in range(3):
                    v.scalar_tensor_tensor(rs_a[:, :], rstd[:, :], -0.5, var[:, :], ALU.mult, ALU.mult)
                    order()
                    v.tensor_tensor(rs_b[:, :], rs_a[:, :], rstd[:, :], ALU.mult)
                    order()
                    v.scalar_tensor_tensor(rstd[:, :], rs_b[:, :], 1.5, rstd[:, :], ALU.add, ALU.mult)
                    order()
                for j in range(HALF):
                    last = v.tensor_scalar(dst[:, j, :], src(j), mean_var[:, j, 0:1], rstd[:, j:j + 1],
                                           ALU.subtract, ALU.mult)
                return last

            with dve.Fori(0, B) as b:
                for h in range(HALVES):
                    t0 = (b * HALVES + h) * HALF

                    def x_tile(j):
                        return x_all[:, bass.ds(t0 + j, 1), :].rearrange("p a e -> p (a e)")

                    def x1_tile(j):
                        return rows[:, bass.ds(t0 + j, 1), 0, :].rearrange("p a e -> p (a e)")

                    norm(x_tile, xn[h]).then_inc(dve_xn, 1)
                    dve.wait_ge(pool_eq, each(b, h, 1, 1))
                    v.scalar_tensor_tensor(q_t[h][:, :], ps[:, 0, :], 0.0, e_q[h][:, :], ALU.max,
                                           ALU.add).then_inc(dve_q, 1)
                    dve.wait_ge(pool_ek, each(b, h, 1, 1))
                    v.scalar_tensor_tensor(k_t[h][:, :], ps[:, 1, :], 0.0, e_k[h][:, :], ALU.max,
                                           ALU.add).then_inc(dve_k, 1)
                    for n in range(2):
                        dve.wait_ge(pool_ekt, each(b, h, 2, n + 1))
                        dve.wait_ge(act_vt, each(b, h, 2, n + 1))
                        kv = ps[:, 2 + n, :].rearrange("p (t c) -> p t c", t=2)
                        v.scalar_tensor_tensor(k_tok[h][:, 2 * n:2 * n + 2, :], kv[:, :, 0:P], 0.0,
                                               e_kt[h][:, 2 * n:2 * n + 2, :], ALU.max, ALU.add).then_inc(dve_kt, 1)
                    dve.wait_ge(act_qhi, each(b, h, 1, 1))
                    v.tensor_tensor(q_lo[h][:, :], q_t[h][:, :], q_hi[h][:, :], ALU.subtract).then_inc(dve_qlo, 1)
                    dve.wait_ge(act_khi, each(b, h, 1, 1))
                    v.tensor_tensor(k_lo[h][:, :], k_t[h][:, :], k_hi[h][:, :], ALU.subtract).then_inc(dve_klo, 1)
                    for k in range(HG):
                        last = v.tensor_scalar(kx_hi[h][:, :, k, :], k_hi[h][:, :].rearrange("p (c m) -> p c m", m=CHUNK),
                                               head_mask[:, k:k + 1], None, ALU.mult)
                    last.then_inc(dve_kx, 1)
                    for r in range(GROUPS):
                        dve.wait_ge(pe_qk, each(b, h, GROUPS, r + 1))
                        v.tensor_tensor(attn[h][:, r, :, :], ps[:, r % 2, :].rearrange("p (c l) -> p c l", l=CHUNK),
                                        causal[:, :].unsqueeze(1).broadcast_to([P, CPH, CHUNK]),
                                        ALU.mult).then_inc(dve_at, 1)
                        dve.wait_ge(pe_ds, each(b, h, HALF, r + 1))
                        v.tensor_tensor(part[h][:, r, :, :].rearrange("p (a c) o -> p a c o", a=2),
                                        ps[:, 4:6, 0:2 * OW].rearrange("p a (c o) -> p a c o", c=2),
                                        state_mask[:, :].unsqueeze(1).unsqueeze(1).broadcast_to([P, 2, 2, OW]),
                                        ALU.mult).then_inc(dve_sm, 1)
                        order()
                        before_tile = state[h][:, r, :] if (r or not h) else state[0][:, HALF, :]
                        v.tensor_tensor(state[h][:, r + 1, :], before_tile, part[h][:, r, CPT - 1, :],
                                        ALU.add).then_inc(dve_st, 1)
                        order()
                    for j in range(HALF):
                        o_ps = ps[:, 6 if j % 2 == 0 else 2, 0:OW].rearrange("p (g c) -> p g c", g=GROUPS)
                        dve.wait_ge(pe_o, each(b, h, HALF, j + 1))
                        v.tensor_scalar(den[0][:, :].rearrange("p (g k) -> p g k", g=GROUPS), o_ps[:, :, NUM:GW],
                                        1e-6, None, ALU.max)
                        order()
                        v.reciprocal(rden[0][:, :], den[0][:, :])
                        order()
                        v.tensor_tensor(
                            heads_out[h][:, j, :].rearrange("p (g k d) -> p g k d", g=GROUPS, k=HG),
                            o_ps[:, :, 0:NUM].rearrange("p g (k d) -> p g k d", k=HG),
                            rden[0][:, :].rearrange("p (g k) -> p g k", g=GROUPS).unsqueeze(3)
                            .broadcast_to([P, GROUPS, HG, D]), ALU.mult).then_inc(dve_ao, 1)
                        order()
                    dve.wait_ge(pe_y, each(b, h, 1, 1))
                    v.tensor_tensor(rows[:, bass.ds(t0, HALF), 0, :], ps[:, 3, :].rearrange("p (t e) -> p t e", e=E),
                                    x_all[:, bass.ds(t0, HALF), :], ALU.add).then_inc(dve_x1, 1)
                    order()
                    norm(x1_tile, xn[h]).then_inc(dve_xn2, 1)
                    dve.wait_ge(pool_h2, each(b, h, 1, 1))
                    v.tensor_tensor(rt_s[:, :], rows[:, bass.ds(t0, HALF), 1, 0], rows[:, bass.ds(t0, HALF), 1, 1],
                                    ALU.add)
                    order()
                    v.scalar_tensor_tensor(rt_t[:, :], rt_s[:, :], -1.0, rt_s[:, :], ALU.mult, ALU.max)
                    order()
                    v.tensor_copy(rt_i[:, :], rt_t[:, :])
                    v.tensor_scalar(rt_g[:, :], rt_s[:, :], 0.0, 2.0, ALU.is_ge, ALU.mult)
                    order()
                    v.tensor_copy(rt_f[:, :], rt_i[:, :])
                    order()
                    v.tensor_tensor(rt_m[:, :], rt_f[:, :], rt_t[:, :], ALU.is_gt)
                    order()
                    v.tensor_tensor(rt_f[:, :], rt_f[:, :], rt_m[:, :], ALU.subtract)
                    order()
                    v.scalar_tensor_tensor(rt_i[:, :], rt_g[:, :], -1.0, rt_f[:, :], ALU.add, ALU.mult)
                    order()
                    v.tensor_scalar(rt_i2[:, :], rt_i[:, :], EXPERTS - 1, None, ALU.bitwise_and)
                    order()
                    v.tensor_copy(rt_g[:, :], rt_i2[:, :])
                    order()
                    v.tensor_tensor(onehot[:, :, :], iota_row[:, 0:EXPERTS].unsqueeze(1).broadcast_to([P, HALF, EXPERTS]),
                                    rt_g[:, :].unsqueeze(2).broadcast_to([P, HALF, EXPERTS]), ALU.is_equal)
                    order()
                    for j in range(HALF):
                        last = v.tensor_tensor(earlier[:, j + 1, :], earlier[:, j, :], onehot[:, j, :], ALU.add)
                        if j < HALF - 1:
                            order()
                    last.then_inc(dve_oh, 1)
                    dve.wait_ge(pe_rank, each(b, h, 1, 1))
                    v.tensor_copy(earlier[:, 0, :], earlier[:, HALF, :])
                    v.tensor_tensor(rank8[:, :, :], ps[:, 7, 0:HALF * EXPERTS].rearrange("p (t e) -> p t e", e=EXPERTS),
                                    onehot[:, :, :], ALU.mult)
                    order()
                    v.tensor_reduce(rt_r[:, :], rank8[:, :, :], axis=AX.X, op=ALU.add)
                    order()
                    v.tensor_copy(rt_i[:, :], rt_r[:, :])
                    order()
                    v.tensor_scalar(rt_i2[:, :], rt_i[:, :], P - 1, None, ALU.bitwise_and)
                    v.tensor_scalar(rt_i3[:, :], rt_i[:, :], 7, None, ALU.logical_shift_right)
                    order()
                    v.tensor_copy(rt_r[:, :], rt_i2[:, :])
                    v.tensor_copy(rt_k[:, :], rt_i3[:, :])
                    order()
                    v.scalar_tensor_tensor(rt_k[:, :], rt_g[:, :], float(PLACES), rt_k[:, :], ALU.mult, ALU.add)
                    v.tensor_tensor(oh_place[:, :, :], iota_row[:, :].unsqueeze(1).broadcast_to([P, HALF, P]),
                                    rt_r[:, :].unsqueeze(2).broadcast_to([P, HALF, P]), ALU.is_equal)
                    order()
                    for j in range(HALF):
                        last = v.tensor_scalar(oh_token[:, j, :], iota_row[:, :], rt_k[:, j:j + 1],
                                               token1[:, bass.ds(t0 + j, 1)], ALU.is_equal, ALU.mult)
                    last.then_inc(dve_v, 1)
                    dve.wait_ge(pe_perm, each(b, h, 1, 1))
                    v.tensor_tensor(table[:, :], table[:, :], ps[:, 7, 0:P], ALU.add).then_inc(dve_perm, 1)
                    order()

            v.tensor_copy(table16[:, :], table[:, :]).then_inc(dve_run, 1)
            dve.wait_ge(pe_total, 1)
            v.tensor_scalar(total[:, :], ps[:, 7, 0:EXPERTS], float(P - 1), None, ALU.add)
            order()
            v.tensor_copy(tot_i[:, :], total[:, :])
            order()
            v.tensor_scalar(tot_i[:, :], tot_i[:, :], 7, None, ALU.logical_shift_right)
            order()
            v.tensor_copy(tiles_of[:, :], tot_i[:, :])
            order()
            v.tensor_copy(ends[:, 0:1], tiles_of[:, 0:1])
            order()
            for e in range(1, EXPERTS):
                v.tensor_tensor(ends[:, e:e + 1], ends[:, e - 1:e], tiles_of[:, e:e + 1], ALU.add)
                order()
            all_s = [P, SLOTS, EXPERTS]
            v.tensor_tensor(passed[:, :, :], ends[:, :].unsqueeze(1).broadcast_to(all_s),
                            iota_row[:, 0:SLOTS].unsqueeze(2).broadcast_to(all_s), ALU.is_le)
            order()
            v.tensor_tensor(weighed[:, :, :], passed[:, :, :], tiles_of[:, :].unsqueeze(1).broadcast_to(all_s), ALU.mult)
            v.tensor_reduce(slot_g[:, :], passed[:, :, :], axis=AX.X, op=ALU.add)
            order()
            v.tensor_reduce(slot_b[:, :], weighed[:, :, :], axis=AX.X, op=ALU.add)
            v.tensor_copy(slot_gi[:, :], slot_g[:, :])
            order()
            v.tensor_tensor(slot_c[:, :], iota_row[:, 0:SLOTS], slot_b[:, :], ALU.subtract)
            v.tensor_scalar(slot_gm[:, :], slot_gi[:, :], EXPERTS - 1, None, ALU.bitwise_and)
            order()
            v.scalar_tensor_tensor(slot_c[:, :], slot_g[:, :], float(PLACES), slot_c[:, :], ALU.mult, ALU.add)
            order()
            v.tensor_scalar(pick[:, :], slot_c[:, :], part_f[:, 0:1], None, ALU.is_equal).then_inc(dve_pick, 1)
            dve.wait_ge(pe_slots, 1)
            v.tensor_copy(tok_f[:, :], ps[:, 6, 0:SLOTS])
            order()
            v.tensor_scalar(tok_e[:, :], tok_f[:, :], 0.5, part_far[:, 0:1], ALU.is_lt, ALU.mult)
            v.tensor_scalar(src_f[:, :], tok_f[:, :], -1.0, 0.0, ALU.add, ALU.max)
            v.tensor_scalar(second[:, :], tok_f[:, :], L + 0.5, None, ALU.is_gt)
            v.tensor_scalar(first[:, :], tok_f[:, :], L + 0.5, None, ALU.is_lt)
            order()
            v.tensor_copy(src_i[:, :], src_f[:, :])
            v.tensor_tensor(dst_f[:, :], tok_e[:, :], src_f[:, :], ALU.add)
            order()
            v.tensor_copy(dst_i[:, :], dst_f[:, :])
            order()
            dve.wait_ge(in_w1, 16 * (EXPERTS + 1))
            v.memset(den[1][:, :], 0.0).then_inc(dve_slots, 1)

            with dve.Fori(0, SLOTS) as n:
                expert = dve.value_load(slot_gm[0:1, bass.ds(n, 1)], min_val=0, max_val=EXPERTS - 1)
                v.tensor_copy(w1_now[:, :, :], w1[:, bass.ds(expert, 2), :]).then_inc(dve_w1, 1)
                v.tensor_scalar(gate_a[:, :], gates[:, 1, 1, :], second[:, bass.ds(n, 1)], None, ALU.mult)
                order()
                v.scalar_tensor_tensor(gate_b[:, :], gates[:, 0, 1, :], first[:, bass.ds(n, 1)], gate_a[:, :],
                                       ALU.mult, ALU.add)
                dve.wait_ge(pe_w1, n * 2 + 2)
                for c in range(FC):
                    last = v.tensor_scalar(hid[:, 1, c, :], ps[:, 1, c * P:(c + 1) * P],
                                           b1[:, bass.ds(expert * FC + (FC + c), 1)], 0.0, ALU.add, ALU.max)
                last.then_inc(dve_hid, 1)
                dve.wait_ge(pe_y2, n + 1)
                v.tensor_tensor(y_b[:, :], ps[:, 2, 0:E],
                                b2_pair[:, bass.ds(expert, 1), :].rearrange("p a e -> p (a e)"), ALU.add)
                order()
                v.tensor_tensor(y_g[:, :], y_b[:, :], gate_b[:, :], ALU.mult)
                order()
                v.tensor_tensor(got[:, bass.ds(n, 1), 0, :].rearrange("p a e -> p (a e)"), y_g[:, :],
                                got[:, bass.ds(n, 1), 0, :].rearrange("p a e -> p (a e)"), ALU.add).then_inc(dve_done, 1)

        @block.tensor
        def _(pe):
            def mm(out, lhsT, rhs, start=True, stop=True, **k):
                return nc.tensor.matmul(out, lhsT, rhs, start=start, stop=stop, **k)

            def tr(out, src, n=P):
                return nc.tensor.transpose(out, src, ident[0:n, 0:n])

            pe.wait_ge(const, 1)
            pe.wait_ge(in_small, 80)
            tr(ps[:, 0, 0:B], c_rows[0:B, :], B)
            for k in range(3):
                tr(ps[:, 1, k * P:(k + 1) * P], wqkv[:, k, :])
            tr(ps[:, 2, 0:P], wout[:, :])
            tr(ps[:, 3, 0:EXPERTS * FC], b1_rows[0:EXPERTS * FC, :], EXPERTS * FC).then_inc(setup_pe, 1)
            pe.wait_ge(setup_dve, 1)
            for k in range(2):
                mm(ps[:, 4, k * B:(k + 1) * B], wmod[:, k * E:(k + 1) * E], silu[:, :])
            for b in range(B):
                last = mm(ps[:, 5 + b, :], silu_bc[:, b, :], wmod[:, 2 * E:])
            last.then_inc(setup_pe, 1)
            pe.wait_ge(consts, 1)

            with pe.Fori(0, B) as b:
                for h in range(HALVES):
                    pe.wait_ge(dve_xn, each(b, h, 1, 1))
                    for j in range(HALF):
                        last = tr(ps[:, 7, j * P:(j + 1) * P], xn[h][:, j, :])
                    last.then_inc(pe_xT, 1)
                    pe.wait_ge(act_h, each(b, h, 1, 1))
                    mm(ps[:, 0, :], w_t[:, 0:E], h_t[h][:, :]).then_inc(pe_q, 1)
                    mm(ps[:, 1, :], w_t[:, E:2 * E], h_t[h][:, :]).then_inc(pe_k, 1)
                    mm(ps[:, 4, :], w_t[:, 2 * E:], h_t[h][:, :]).then_inc(pe_vT, 1)
                    for j in range(HALF):
                        last = mm(ps[:, 2 + j // 2, (j % 2) * 256:(j % 2) * 256 + 256], h_t[h][:, j * P:(j + 1) * P],
                                  w_t[:, E:])
                        if j % 2:
                            last.then_inc(pe_kv, 1)
                    pe.wait_ge(pool_vTx, each(b, h, 1, 1))
                    for f in range(CPH // 4):
                        if f >= 2:
                            pe.wait_ge(act_vx, each(b, h, CPH // 4, f - 1))
                        for i in range(4):
                            last = tr(ps[:, 6 + f % 2, i * P:(i + 1) * P],
                                      vx_t[h][:, 4 * f + i, :, :].rearrange("p k m -> p (k m)"))
                        last.then_inc(pe_vx, 1)
                    pe.wait_ge(dve_qlo, each(b, h, 1, 1))
                    pe.wait_ge(dve_kx, each(b, h, 1, 1))
                    pe.wait_ge(pool_kx, each(b, h, 1, 1))
                    pe.wait_ge(dve_kt, each(b, h, 2, 2))
                    for r in range(GROUPS):
                        rp = slice(r * CHUNK, (r + 1) * CHUNK)
                        if r >= 2:
                            pe.wait_ge(dve_at, each(b, h, GROUPS, r - 1))
                        for c in range(CPH):
                            o = ps[:, r % 2, c * CHUNK:(c + 1) * CHUNK]
                            cs = slice(c * CHUNK, (c + 1) * CHUNK)
                            hi = kx_hi[h][rp, c, :, :].rearrange("p k m -> p (k m)")
                            lo = kx_lo[h][rp, c, :, :].rearrange("p k m -> p (k m)")
                            mm(o, hi, q_hi[h][rp, cs], stop=False)
                            mm(o, hi, q_lo[h][rp, cs], start=False, stop=False)
                            last = mm(o, lo, q_hi[h][rp, cs], start=False)
                        last.then_inc(pe_qk, 1)
                        if r:
                            pe.wait_ge(dve_sm, each(b, h, HALF, r))
                        for c in range(CPT):
                            n = (c + 1) * CHUNK
                            last = mm(ps[:, 4 + c // 2, (c % 2) * OW:(c % 2 + 1) * OW], k_tok[h][0:n, r, :],
                                      v_tok[h][0:n, r, :, :].rearrange("p g c -> p (g c)"))
                        last.then_inc(pe_ds, 1)
                    pe.wait_ge(act_vx, each(b, h, CPH // 4, CPH // 4))
                    pe.wait_ge(dve_at, each(b, h, GROUPS, GROUPS))
                    for j in range(HALF):
                        pe.wait_ge(dve_st, each(b, h, HALF, j + 1))
                        if j >= 2:
                            pe.wait_ge(dve_ao, each(b, h, HALF, j - 1))
                        bank = 6 if j % 2 == 0 else 2
                        at_start = state[h][:, j, :] if (j or not h) else state[0][:, HALF, :]
                        mm(ps[:, bank, 0:OW], q_t[h][:, j * P:(j + 1) * P], at_start, stop=False,
                           skip_group_check=True)
                        for c in range(1, CPT):
                            t = j * P + c * CHUNK
                            mm(ps[c * CHUNK:(c + 1) * CHUNK, bank, 0:OW], q_t[h][:, t:t + CHUNK],
                               part[h][:, j, c - 1, :], start=False, stop=False, skip_group_check=True)
                        for c in range(CPT):
                            for r in range(GROUPS):
                                last = mm(ps[c * CHUNK:(c + 1) * CHUNK, bank, r * GW:(r + 1) * GW],
                                          attn[h][:, r, j * CPT + c, :], vx[h][:, j * CPT + c, r, :],
                                          start=False, stop=True, skip_group_check=True)
                        last.then_inc(pe_o, 1)
                    pe.wait_ge(dve_ao, each(b, h, HALF, HALF))
                    for j in range(HALF):
                        last = tr(ps[:, 7, j * P:(j + 1) * P], heads_out[h][:, j, :])
                    last.then_inc(pe_aT, 1)
                    pe.wait_ge(act_aT, each(b, h, 1, 1))
                    for j in range(HALF):
                        last = mm(ps[:, 3, j * P:(j + 1) * P], a_t[h][:, j * P:(j + 1) * P],
                                  wo_g[:, bass.ds(b, 1), :].rearrange("p a e -> p (a e)"))
                    last.then_inc(pe_y, 1)
                    pe.wait_ge(dve_oh, each(b, h, 1, 1))
                    mm(ps[:, 7, 0:HALF * EXPERTS], before[:, :], onehot[:, :, :].rearrange("p t e -> p (t e)"), stop=False)
                    mm(ps[:, 7, 0:HALF * EXPERTS], ones[:, :], earlier[:, 0:HALF, :].rearrange("p t e -> p (t e)"),
                       start=False).then_inc(pe_rank, 1)
                    pe.wait_ge(dve_v, each(b, h, 1, 1))
                    for j in range(HALF):
                        last = mm(ps[:, 7, 0:P], oh_token[:, j, :], oh_place[:, j, :], start=(j == 0), stop=(j == HALF - 1))
                    last.then_inc(pe_perm, 1)
                    pe.wait_ge(dve_perm, each(b, h, 1, 1))

            pe.wait_ge(dve_run, 1)
            mm(ps[:, 7, 0:EXPERTS], ones[:, :], earlier[:, 0, :]).then_inc(pe_total, 1)
            pe.wait_ge(dve_pick, 1)
            mm(ps[:, 6, 0:SLOTS], table16[:, :], pick[:, :]).then_inc(pe_slots, 1)

            pe.wait_ge(in_w2, 16 * (EXPERTS + 1))
            pe.wait_ge(dve_slots, 1)
            with pe.Fori(0, SLOTS) as n:
                expert = pe.value_load(slot_gm[0:1, bass.ds(n, 1)], min_val=0, max_val=EXPERTS - 1)
                pe.wait_ge(act_row, n + 1)
                tr(ps[:, 4, 0:P], h_row[:, :]).then_inc(pe_hT, 1)
                pe.wait_ge(act_hT, n + 1)
                pe.wait_ge(dve_w1, n + 1)
                for x in range(2):
                    for c in range(FC):
                        last = mm(ps[:, x, c * P:(c + 1) * P], w1_now[:, x, c * P:(c + 1) * P], h_col[:, :])
                    last.then_inc(pe_w1, 1)
                for x in range(2):
                    pe.wait_ge((act_hid, dve_hid)[x], n + 1)
                    for c in range(FC):
                        last = mm(ps[:, 2, 0:E], hid[:, x, c, :],
                                  w2[:, bass.ds(expert + x, 1), c, :].rearrange("p a e -> p (a e)"),
                                  start=(x == 0 and c == 0), stop=(x == 1 and c == FC - 1))
                last.then_inc(pe_y2, 1)
                pe.wait_ge(dve_done, n + 1)


_INS = ["L0_attn_x", "L0_attn_W_qkv", "L0_attn_W_out", "L0_ffn_W1", "L0_ffn_b1", "L0_ffn_W2", "L0_ffn_b2",
        "L0_c", "L0_wmod"]


def kernel(**inputs):
    import numpy as np
    import concourse.bacc as bacc
    from concourse.bass_utils import run_bass_kernel_spmd

    nc = bacc.Bacc("TRN2", target_bir_lowering=False, num_devices=1)
    arrays, aps = {}, []
    for name in _INS:
        a = np.ascontiguousarray(inputs[name])
        if name == "L0_attn_x":
            a = a.reshape(B * L, E)
        arrays[f"in_{name}"] = a
        aps.append(nc.dram_tensor(f"in_{name}", a.shape, mybir.dt.from_np(a.dtype), kind="ExternalInput").ap())
    out = nc.dram_tensor("out_rows", (B * L, E), F32, kind="ExternalOutput").ap()
    build(nc, *aps, out)
    r = run_bass_kernel_spmd(nc, [arrays], core_ids=[0])
    return r.results[0]["out_rows"].reshape(B, L, E)
```

```python
from contextlib import ExitStack

import concourse.bass as bass
from concourse import mybir

F32 = mybir.dt.float32
F16 = mybir.dt.float16
I32 = mybir.dt.int32
ALU = mybir.AluOpType
ACT = mybir.ActivationFunctionType
AX = mybir.AxisListType

P = 128
B, L, E = 2, 1024, 128
HEADS = 16
D = E // HEADS
CHUNK = 32
HALF = 4
HALVES = L // (P * HALF)
STEPS = B * HALVES
TILES = B * L // P
CPT = P // CHUNK
CPH = HALF * CPT
HG = P // CHUNK
GROUPS = HEADS // HG
GW = HG * D + HG
NUM = HG * D
OW = GROUPS * GW
EXPERTS = 8
FF = 512
FC = FF // P
SLOTS = TILES + EXPERTS - 1
PLACES = TILES
NO_PLACE = EXPERTS * PLACES
LN_EPS = 1e-5
SCALE = float(D) ** -0.5
RSQRT_SEED = float(0x5F3759DF)
W = HALF * P


def build(nc, x_d, wqkv_d, wout_d, w1_d, b1_d, w2_d, b2_d, c_d, wmod_d, out_d):
    rows_d = nc.dram_tensor("rows_x1_h2", (B * L, 2 * E), F32, kind="Internal").ap()
    with ExitStack() as ctx:
        def sb(name, shape, dtype=F32):
            return ctx.enter_context(nc.sbuf_tensor(name, [P, *shape], dtype))

        def sem(name):
            return ctx.enter_context(nc.semaphore(name))

        ps = ctx.enter_context(nc.psum_tensor("ps", [P, 8, 512], F32))

        x_all = sb("x_all", [TILES, E])
        wqkv = sb("wqkv", [3, E])
        wout = sb("wout", [E])
        w_t = sb("w_t", [3 * E])
        wo_t = sb("wo_t", [E])
        wo_g = sb("wo_g", [B, E])
        wmod = sb("wmod", [6 * E])
        c_rows = sb("c_rows", [P])
        c_t = sb("c_t", [B])
        silu = sb("silu", [B])
        silu_tmp = sb("silu_tmp", [B])
        silu_bc = sb("silu_bc", [B, P])
        col_sa = sb("col_sa", [B])
        col_ca1 = sb("col_ca1", [B])
        row_mod = sb("row_mod", [B, 4, E])
        gates = sb("gates", [B, 2, E])
        row_cb1 = sb("row_cb1", [B, E])
        w1 = sb("w1", [EXPERTS + 1, FF])
        w2 = sb("w2", [EXPERTS + 1, FC, E])
        b1_rows = sb("b1_rows", [P])
        b1 = sb("b1", [(EXPERTS + 1) * FC])
        b2_pair = sb("b2_pair", [EXPERTS, E])

        ident = sb("ident", [P])
        before = sb("before", [P], F16)
        ones = sb("ones", [P], F16)
        causal = sb("causal", [CHUNK])
        iota_row = sb("iota_row", [P])
        part_i = sb("part_i", [1], I32)
        part_f = sb("part_f", [1])
        part_far = sb("part_far", [1])
        part_i2 = sb("part_i2", [3], I32)
        part_f2 = sb("part_f2", [3])
        token1 = sb("token1", [TILES])
        col_head = sb("col_head", [GROUPS, GW])
        state_mask = sb("state_mask", [OW])
        head_mask = sb("head_mask", [HG])
        den_mask = sb("den_mask", [HG])

        def two(name, shape, dtype=F32):
            return [sb(f"{name}{h}", shape, dtype) for h in range(2)]

        def one(name, shape, dtype=F32):
            return [sb(name, shape, dtype)] * 2

        stats = sb("stats", [HALF, 6])
        mean_var = sb("mean_var", [HALF, 2])
        var = sb("var", [HALF])
        rs_a = sb("rs_a", [HALF])
        rs_b = sb("rs_b", [HALF])
        rstd = sb("rstd", [HALF])
        xn = two("xn", [HALF, E])
        h_t = one("h_t", [W])
        e_q = one("e_q", [W])
        e_k = one("e_k", [W])
        e_kt = one("e_kt", [HALF, P])
        arena = sb("arena", [SLOTS * 2 * E])
        q_t = [arena[:, h * W:(h + 1) * W] for h in range(2)]
        k_t = one("k_t", [W])
        q_hi = two("q_hi", [W], F16)
        q_lo = two("q_lo", [W], F16)
        k_hi = one("k_hi", [W], F16)
        k_lo = one("k_lo", [W], F16)
        kx_all = sb("kx_all", [2, 2, CPH, HG, CHUNK], F16)
        kx_hi = [kx_all[:, 0, h, :, :, :] for h in range(2)]
        kx_lo = [kx_all[:, 1, h, :, :, :] for h in range(2)]
        k_tok = two("k_tok", [HALF, P])
        v_tok = two("v_tok", [HALF, GROUPS, GW])
        vx_t = one("vx_t", [CPH, HG, CHUNK])
        vx = [arena[:, 2 * W + h * CPH * OW:2 * W + (h + 1) * CPH * OW]
              .rearrange("p (c g n) -> p c g n", c=CPH, g=GROUPS) for h in range(2)]
        attn = one("attn", [GROUPS, CPH, CHUNK])
        flat = attn[0][:, :, :, :].rearrange("p g c l -> p (g c l)")
        gate_abs = flat[:, 0:B * 2 * E].rearrange("p (b k e) -> p b k e", b=B, k=2)
        gate_sgn = flat[:, B * 2 * E:2 * B * 2 * E].rearrange("p (b k e) -> p b k e", b=B, k=2)
        part = one("part", [HALF, CPT, OW])
        b2 = part[0][:, :, :, :].rearrange("p t c o -> p (t c o)")[:, 0:(EXPERTS + 1) * E] \
            .rearrange("p (e d) -> p e d", d=E)
        state = two("state", [HALF + 1, OW])
        den = two("den", [HEADS])
        rden = two("rden", [HEADS])
        heads_out = one("heads_out", [HALF, E])
        a_t = one("a_t", [W])
        rows = two("rows", [HALF, 2, E])
        xn2 = one("xn2", [HALF, E])
        rt_s = sb("rt_s", [HALF])
        rt_t = sb("rt_t", [HALF])
        rt_i = sb("rt_i", [HALF], I32)
        rt_f = sb("rt_f", [HALF])
        rt_m = sb("rt_m", [HALF])
        rt_g = sb("rt_g", [HALF])
        rt_r = sb("rt_r", [HALF])
        rt_k = sb("rt_k", [HALF])
        rt_i2 = sb("rt_i2", [HALF], I32)
        rt_i3 = sb("rt_i3", [HALF], I32)
        onehot = sb("onehot", [HALF, EXPERTS], F16)
        earlier = sb("earlier", [HALF + 1, EXPERTS], F16)
        rank8 = sb("rank8", [HALF, EXPERTS])
        oh_place = sb("oh_place", [HALF, P], F16)
        oh_token = sb("oh_token", [HALF, P], F16)
        table = sb("table", [P])
        table16 = sb("table16", [P], F16)
        total = sb("total", [EXPERTS])
        tot_i = sb("tot_i", [EXPERTS], I32)
        tiles_of = sb("tiles_of", [EXPERTS])
        ends = sb("ends", [EXPERTS])
        passed = sb("passed", [SLOTS, EXPERTS])
        weighed = sb("weighed", [SLOTS, EXPERTS])
        slot_g = sb("slot_g", [SLOTS])
        slot_b = sb("slot_b", [SLOTS])
        slot_c = sb("slot_c", [SLOTS])
        slot_gi = sb("slot_gi", [SLOTS], I32)
        slot_gm = sb("slot_gm", [SLOTS], I32)
        pick = sb("pick", [SLOTS], F16)
        tok_f = sb("tok_f", [SLOTS])
        tok_e = sb("tok_e", [SLOTS])
        src_f = sb("src_f", [SLOTS])
        src_i = sb("src_i", [SLOTS], I32)
        dst_f = sb("dst_f", [SLOTS])
        dst_i = sb("dst_i", [SLOTS], I32)
        second = sb("second", [SLOTS])
        first = sb("first", [SLOTS])
        got = arena[:, :].rearrange("p (n a e) -> p n a e", n=SLOTS, a=2)
        h_row = two("h_row", [E])
        h_col = two("h_col", [P])
        w1_now = [flat[:, k * 2 * FF:(k + 1) * 2 * FF].rearrange("p (x f) -> p x f", x=2) for k in range(2)]
        hid = [part[0][:, :, :, :].rearrange("p t c o -> p (t c o)")[:, k * 2 * FF:(k + 1) * 2 * FF]
               .rearrange("p (x c t) -> p x c t", x=2, c=FC) for k in range(2)]
        b2_now = kx_all[:, :, :, :, :, :].rearrange("p a h c k m -> p (a h c k m)").bitcast(F32)[:, 0:SLOTS * E] \
            .rearrange("p (n e) -> p n e", n=SLOTS)
        b1_now = sb("b1_now", [SLOTS, 2 * FC])
        y_b = sb("y_b", [E])
        gate_a = sb("gate_a", [E])
        gate_b = sb("gate_b", [E])
        y_g = sb("y_g", [E])
        done = got[:, :, 0, :]

        in_small = sem("in_small")
        in_x0 = sem("in_x0")
        in_x = sem("in_x")
        in_w1 = sem("in_w1")
        in_w2 = sem("in_w2")
        in_b2 = sem("in_b2")
        const = sem("const")
        consts = sem("consts")
        setup_pe = sem("setup_pe")
        setup_act = sem("setup_act")
        setup_dve = sem("setup_dve")
        pe_xT = sem("pe_xT")
        pe_q = sem("pe_q")
        pe_k = sem("pe_k")
        pe_vT = sem("pe_vT")
        pe_kv = sem("pe_kv")
        pe_vx = sem("pe_vx")
        pe_qk = sem("pe_qk")
        pe_ds = sem("pe_ds")
        pe_o = sem("pe_o")
        pe_aT = sem("pe_aT")
        pe_y = sem("pe_y")
        pe_rank = sem("pe_rank")
        pe_perm = sem("pe_perm")
        act_h = sem("act_h")
        act_eq = sem("act_eq")
        act_ek = sem("act_ek")
        act_vTx = sem("act_vTx")
        act_kx = sem("act_kx")
        act_ekt = sem("act_ekt")
        act_vt = sem("act_vt")
        act_qhi = sem("act_qhi")
        act_khi = sem("act_khi")
        act_vx = sem("act_vx")
        act_aT = sem("act_aT")
        pool_eq = sem("pool_eq")
        pool_ek = sem("pool_ek")
        pool_ekt = sem("pool_ekt")
        pool_h2 = sem("pool_h2")
        dve_xn = sem("dve_xn")
        dve_q = sem("dve_q")
        dve_k = sem("dve_k")
        dve_kt = sem("dve_kt")
        dve_qlo = sem("dve_qlo")
        dve_klo = sem("dve_klo")
        dve_kx = sem("dve_kx")
        dve_at = sem("dve_at")
        dve_sm = sem("dve_sm")
        dve_st = sem("dve_st")
        dve_ao = sem("dve_ao")
        dve_x1 = sem("dve_x1")
        dve_xn2 = sem("dve_xn2")
        dve_oh = sem("dve_oh")
        dve_v = sem("dve_v")
        dve_perm = sem("dve_perm")
        dve_run = sem("dve_run")
        pe_total = sem("pe_total")
        dve_pick = sem("dve_pick")
        pe_slots = sem("pe_slots")
        dve_slots = sem("dve_slots")
        rows_out = sem("rows_out")
        gathered_even = sem("gathered_even")
        gathered_odd = sem("gathered_odd")
        gathered = (gathered_even, gathered_odd)
        act_row = sem("act_row")
        pe_hT = sem("pe_hT")
        act_hT = sem("act_hT")
        pe_w1 = sem("pe_w1")
        act_hid = sem("act_hid")
        dve_hid = sem("dve_hid")
        pe_y2 = sem("pe_y2")
        act_w1 = sem("act_w1")
        y_free = sem("y_free")
        turns = sem("turns")
        dve_done = sem("dve_done")
        scattered = sem("scattered")
        b2_ready = sem("b2_ready")

        def wait_alone(eng, semaphore, value):
            eng.wait_ge(semaphore, value)
            eng.sem_inc(turns, 1)

        TURNS = range(-1, STEPS + 1)

        def parts_of(u):
            return u + 1 < STEPS, 0 <= u < STEPS, u > 0

        block = ctx.enter_context(nc.Block())

        @block.sync
        def _(sp):
            with nc.allow_non_contiguous_dma(reason="rows of experts"):
                sp.dma_start(x_all[:, 0:HALF, :], x_d[0:W, :].rearrange("(t p) e -> p t e", p=P)).then_inc(in_x0, 16)
                sp.dma_start(c_rows[0:B, :], c_d).then_inc(in_small, 16)
                sp.dma_start(wqkv[:, :, :], wqkv_d.rearrange("(g o) e -> o g e", o=P)).then_inc(in_small, 16)
                sp.dma_start(wmod[:, :], wmod_d).then_inc(in_small, 16)
                sp.dma_start(wout[:, :], wout_d).then_inc(in_small, 16)
                sp.dma_start(b1_rows[0:EXPERTS * FC, :], b1_d.rearrange("e (c p) -> (e c) p", p=P)).then_inc(in_small, 16)
                sp.dma_start(x_all[:, HALF:, :], x_d[W:, :].rearrange("(t p) e -> p t e", p=P)).then_inc(in_x, 16)
                sp.dma_start(b2[:, 0:EXPERTS, :], b2_d.rearrange("e d -> (e d)").partition_broadcast(P)
                             .rearrange("p (e d) -> p e d", d=E)).then_inc(in_b2, 16)
                sp.dma_start(b2[:, EXPERTS, :], b2_d[0, :].partition_broadcast(P)).then_inc(in_b2, 16)
                w1_v = w1_d.rearrange("e d f -> d e f")
                w2_v = w2_d.rearrange("e (c p) d -> p e c d", p=P)
                for e in range(EXPERTS):
                    sp.dma_start(w1[:, e, :], w1_v[:, e, :]).then_inc(in_w1, 16)
                    sp.dma_start(w2[:, e, :, :], w2_v[:, e, :, :]).then_inc(in_w2, 16)
                sp.dma_start(w1[:, EXPERTS, :], w1_v[:, 0, :]).then_inc(in_w1, 16)
                sp.dma_start(w2[:, EXPERTS, :, :], w2_v[:, 0, :, :]).then_inc(in_w2, 16)
                for s in range(STEPS):
                    sp.wait_ge(pool_h2, s + 1)
                    if s:
                        sp.wait_ge(rows_out, 16 * s)
                    sp.dma_start(rows_d[s * W:(s + 1) * W, :].rearrange("(t p) c -> p t c", p=P),
                                 rows[s % 2][:, :, :, :].rearrange("p t a e -> p t (a e)")).then_inc(rows_out, 16)
                sp.wait_ge(rows_out, 16 * STEPS)

        @block.gpsimd
        def _(pool):
            g = nc.gpsimd
            g.memset(ident[:, :], 0.0)
            g.memset(before[:, :], 1.0)
            g.memset(ones[:, :], 1.0)
            g.memset(causal[:, :], SCALE)
            imprecise = dict(allow_small_or_imprecise_dtypes=True)
            g.iota(iota_row[:, :], pattern=[[1, P]], base=0, channel_multiplier=0, **imprecise)
            g.iota(part_i[:, :], pattern=[[1, 1]], base=0, channel_multiplier=1)
            g.iota(part_f[:, :], pattern=[[1, 1]], base=0, channel_multiplier=1, **imprecise)
            g.iota(token1[:, :], pattern=[[P, TILES]], base=1, channel_multiplier=1, **imprecise)
            g.iota(col_head[:, :, 0:NUM].rearrange("p g (h d) -> p g h d", d=D),
                   pattern=[[HG, GROUPS], [1, HG], [0, D]], base=0, channel_multiplier=0, **imprecise)
            g.iota(col_head[:, :, NUM:GW], pattern=[[HG, GROUPS], [1, HG]], base=0, channel_multiplier=0,
                   **imprecise)
            pool.drain()
            g.affine_select(out=ident[:, :], in_=ident[:, :], compare_op=ALU.not_equal, fill=1.0, base=0,
                            pattern=[[-1, P]], channel_multiplier=1)
            g.affine_select(out=before[:, :], in_=before[:, :], compare_op=ALU.is_gt, fill=0.0, base=0,
                            pattern=[[1, P]], channel_multiplier=-1)
            for k in range(HG):
                pool.drain()
                rows_k = causal[k * CHUNK:(k + 1) * CHUNK, :]
                g.affine_select(out=rows_k, in_=rows_k, compare_op=ALU.is_ge, fill=0.0, base=0,
                                pattern=[[1, CHUNK]], channel_multiplier=-1)
            pool.drain()
            g.memset(state[0][:, 0, :], 0.0).then_inc(const, 1)
            pool.wait_ge(in_b2, 32)
            g.tensor_tensor(b2_pair[:, :, :], b2[:, 0:EXPERTS, :], b2[:, 1:EXPERTS + 1, :], ALU.add).then_inc(b2_ready, 1)

            def min_one(dst):
                return g.tensor_scalar(dst, dst, 1.0, None, ALU.min)

            for u in TURNS:
                has_a, _, has_c = parts_of(u)
                if has_a:
                    s, h = u + 1, (u + 1) % 2
                    pool.wait_ge(act_eq, s + 1)
                    min_one(e_q[h][:, :]).then_inc(pool_eq, 1)
                    pool.wait_ge(act_ek, s + 1)
                    min_one(e_k[h][:, :]).then_inc(pool_ek, 1)
                if has_c:
                    s, h, b = u - 1, (u - 1) % 2, (u - 1) // HALVES
                    pool.wait_ge(dve_xn2, s + 1)
                    g.tensor_tensor(xn2[h][:, :, :], xn2[h][:, :, :],
                                    row_cb1[:, b:b + 1, :].broadcast_to([P, HALF, E]), ALU.mult)
                    pool.drain()
                    g.tensor_tensor(rows[h][:, :, 1, :], xn2[h][:, :, :],
                                    row_mod[:, b:b + 1, 1, :].broadcast_to([P, HALF, E]),
                                    ALU.add).then_inc(pool_h2, 1)
                if has_a:
                    s, h = u + 1, (u + 1) % 2
                    for n in range(2):
                        pool.wait_ge(act_ekt, 2 * s + n + 1)
                        min_one(e_kt[h][:, 2 * n:2 * n + 2, :]).then_inc(pool_ekt, 1)

            pool.wait_ge(rows_out, 16 * STEPS)
            pool.wait_ge(dve_slots, 1)

            def gather(n):
                if n >= 2:
                    pool.wait_ge(gathered[n % 2], 16 * (n // 2))
                g.indirect_dma_start(out=got[:, n, :, :].rearrange("p a e -> p (a e)"), out_offset=None,
                                     in_=rows_d, in_offset=bass.IndirectOffsetOnAxis(ap=src_i[:, n:n + 1], axis=0)
                                     ).then_inc(gathered[n % 2], 16)

            ahead = 4
            for n in range(ahead):
                gather(n)
            for n in range(SLOTS):
                if n + ahead < SLOTS:
                    gather(n + ahead)
                pool.wait_ge(dve_done, n + 1)
                g.indirect_dma_start(out=out_d, out_offset=bass.IndirectOffsetOnAxis(ap=dst_i[:, n:n + 1], axis=0),
                                     in_=done[:, n, :], in_offset=None, bounds_check=B * L - 1, oob_is_err=False
                                     ).then_inc(scattered, 16)
            pool.wait_ge(scattered, 16 * SLOTS)

        @block.scalar
        def _(act):
            a = nc.scalar
            act.wait_ge(setup_pe, 1)
            a.activation(c_t[:, :], ps[:, 0, 0:B], ACT.Copy)
            a.activation(w_t[:, :], ps[:, 1, 0:3 * E], ACT.Copy)
            a.activation(wo_t[:, :], ps[:, 2, 0:E], ACT.Copy)
            a.activation(b1[:, 0:EXPERTS * FC], ps[:, 3, 0:EXPERTS * FC], ACT.Copy)
            a.activation(b1[:, EXPERTS * FC:], ps[:, 3, 0:FC], ACT.Copy)
            act.drain()
            a.activation(silu_tmp[:, :], c_t[:, :], ACT.Exp, scale=-1.0).then_inc(setup_act, 1)
            act.wait_ge(consts, 1)

            for u in TURNS:
                has_a, _, has_c = parts_of(u)
                if has_c:
                    s, h = u - 1, (u - 1) % 2
                    act.wait_ge(pe_aT, s + 1)
                    a.activation(a_t[h][:, :], ps[:, 6, :], ACT.Copy).then_inc(act_aT, 1)
                if has_a:
                    s, h, b = u + 1, (u + 1) % 2, (u + 1) // HALVES
                    act.wait_ge(pe_xT, s + 1)
                    a.activation(h_t[h][:, :], ps[:, 2, :], ACT.Identity, scale=col_ca1[:, b:b + 1],
                                 bias=col_sa[:, b:b + 1]).then_inc(act_h, 1)
                    act.wait_ge(pe_q, s + 1)
                    if s:
                        act.wait_ge(dve_q, s)
                    a.activation(e_q[h][:, :], ps[:, 3, :], ACT.Exp).then_inc(act_eq, 1)
                    act.wait_ge(pe_k, s + 1)
                    if s:
                        act.wait_ge(dve_k, s)
                    a.activation(e_k[h][:, :], ps[:, 2, :], ACT.Exp).then_inc(act_ek, 1)
                    act.wait_ge(pe_vT, s + 1)
                    if s:
                        act.wait_ge(pe_vx, s * CPT)
                    for k in range(HG):
                        last = a.activation(vx_t[h][:, :, k, :], ps[:, 3, :].rearrange("p (c m) -> p c m", m=CHUNK),
                                            ACT.Copy, scale=head_mask[:, k:k + 1])
                    last.then_inc(act_vTx, 1)
                    for n in range(2):
                        kv = ps[:, 2 + n, :].rearrange("p (t c) -> p t c", t=2)
                        act.wait_ge(pe_kv, 2 * s + n + 1)
                        if s:
                            act.wait_ge(dve_kt, 2 * s - 1 + n)
                        a.activation(e_kt[h][:, 2 * n:2 * n + 2, :], kv[:, :, 0:P], ACT.Exp).then_inc(act_ekt, 1)
                        for t in range(2):
                            last = a.activation(v_tok[h][:, 2 * n + t, :, 0:NUM],
                                                kv[:, t, P:].rearrange("p (g c) -> p g c", g=GROUPS), ACT.Copy)
                        last.then_inc(act_vt, 1)
                    act.wait_ge(dve_q, s + 1)
                    a.activation(q_hi[h][:, :], q_t[h][:, :], ACT.Copy).then_inc(act_qhi, 1)
                    act.wait_ge(dve_k, s + 1)
                    a.activation(k_hi[h][:, :], k_t[h][:, :], ACT.Copy).then_inc(act_khi, 1)
                    act.wait_ge(dve_klo, s + 1)
                    for k in range(HG):
                        last = a.activation(kx_lo[h][:, :, k, :], k_lo[h][:, :].rearrange("p (c m) -> p c m", m=CHUNK),
                                            ACT.Copy, scale=head_mask[:, k:k + 1])
                    last.then_inc(act_kx, 1)
                    for f in range(CPH // 4):
                        act.wait_ge(pe_vx, s * CPT + f + 1)
                        a.activation(vx[h][:, 4 * f:4 * f + 4, :, 0:NUM].rearrange("p c g n -> p (c g) n"),
                                     ps[:, 2 + f % 2, :].rearrange("p (c n) -> p c n", n=NUM),
                                     ACT.Copy).then_inc(act_vx, 1)

            def stage_expert(n, k):
                expert = act.value_load(slot_gm[0:1, bass.ds(n, 1)], min_val=0, max_val=EXPERTS - 1)
                a.activation(b1_now[:, bass.ds(n, 1), :].rearrange("p a c -> p (a c)"),
                             b1[:, bass.ds(expert * FC, 2 * FC)], ACT.Copy)
                a.activation(b2_now[:, bass.ds(n, 1), :].rearrange("p a e -> p (a e)"),
                             b2_pair[:, bass.ds(expert, 1), :].rearrange("p a e -> p (a e)"), ACT.Copy)
                a.activation(w1_now[k][:, :, :], w1[:, bass.ds(expert, 2), :], ACT.Copy).then_inc(act_w1, 1)

            def row(n, k):
                a.activation(h_row[k][:, :], got[:, bass.ds(n, 1), 1, :].rearrange("p a e -> p (a e)"),
                             ACT.Copy).then_inc(act_row, 1)

            def column(k):
                a.activation(h_col[k][:, :], ps[:, 6 + k, 0:P], ACT.Copy).then_inc(act_hT, 1)

            def relu_first(n, k):
                for c in range(FC):
                    last = a.activation(hid[k][:, 0, c, :], ps[:, 2 * k, c * P:(c + 1) * P], ACT.Relu,
                                        bias=b1_now[:, bass.ds(n, 1), c])
                last.then_inc(act_hid, 1)

            act.wait_ge(dve_slots, 1)
            act.wait_ge(in_w1, 16 * (EXPERTS + 1))
            act.wait_ge(b2_ready, 1)
            for n in range(2):
                stage_expert(n, n)
            for n in range(2):
                act.wait_ge(gathered[n], 16)
                row(n, n)
                act.wait_ge(pe_hT, n + 1)
                column(n)
            act.drain()
            with act.Fori(0, SLOTS // 2 - 1) as i:
                for k in range(2):
                    n = i * 2 + k
                    wait_alone(act, gathered[k], i * 16 + 32)
                    row(n + 2, k)
                    wait_alone(act, pe_w1, n * 2 + 1)
                    relu_first(n, k)
                    wait_alone(act, pe_w1, n * 2 + 2)
                    stage_expert(n + 2, k)
                    wait_alone(act, pe_hT, n + 3)
                    column(k)
            for n in range(SLOTS - SLOTS % 2 - 2, SLOTS):
                k = n % 2
                if n + 2 < SLOTS:
                    act.wait_ge(gathered[k], 16 * (n // 2 + 2))
                    row(n + 2, k)
                act.wait_ge(pe_w1, 2 * n + 1)
                relu_first(n, k)
                if n + 2 < SLOTS:
                    act.wait_ge(pe_w1, 2 * n + 2)
                    stage_expert(n + 2, k)
                    act.wait_ge(pe_hT, n + 3)
                    column(k)

        @block.vector
        def _(dve):
            v = nc.vector
            order = dve.drain

            def norm(src, dst):
                for j in range(HALF):
                    v.bn_stats(out=stats[:, j, :], in_=src(j))
                order()
                for j in range(HALF):
                    v.bn_aggr(out=mean_var[:, j, :], in_=stats[:, j, :])
                order()
                v.tensor_scalar(var[:, :], mean_var[:, :, 1], LN_EPS, None, ALU.add)
                order()
                v.tensor_scalar(rstd[:, :].bitcast(I32), var[:, :].bitcast(I32), -0.5, RSQRT_SEED, ALU.mult, ALU.add)
                order()
                for _ in range(3):
                    v.scalar_tensor_tensor(rs_a[:, :], rstd[:, :], -0.5, var[:, :], ALU.mult, ALU.mult)
                    order()
                    v.tensor_tensor(rs_b[:, :], rs_a[:, :], rstd[:, :], ALU.mult)
                    order()
                    v.scalar_tensor_tensor(rstd[:, :], rs_b[:, :], 1.5, rstd[:, :], ALU.add, ALU.mult)
                    order()
                for j in range(HALF):
                    last = v.tensor_scalar(dst[:, j, :], src(j), mean_var[:, j, 0:1], rstd[:, j:j + 1],
                                           ALU.subtract, ALU.mult)
                return last

            def norm_x(s):
                norm(lambda j: x_all[:, s * HALF + j, :], xn[s % 2]).then_inc(dve_xn, 1)

            dve.wait_ge(in_x0, 16)
            norm_x(0)
            v.memset(table[:, :], 0.0)
            v.memset(v_tok[0][:, :, :, NUM:GW], 1.0)
            v.memset(v_tok[1][:, :, :, NUM:GW], 1.0)
            v.memset(earlier[:, 0, :], 0.0)
            dve.wait_ge(const, 1)
            v.tensor_scalar(part_i2[:, 0:1], part_i[:, :], 3, None, ALU.logical_shift_right)
            v.tensor_scalar(part_i2[:, 1:2], part_i[:, :], 3, HG - 1, ALU.logical_shift_right, ALU.bitwise_and)
            v.tensor_scalar(part_i2[:, 2:3], part_i[:, :], 5, None, ALU.logical_shift_right)
            order()
            v.tensor_copy(part_f2[:, :], part_i2[:, :])
            v.tensor_scalar(part_far[:, :], part_f[:, :], float(2 * B * L), None, ALU.add)
            order()
            v.tensor_scalar(head_mask[:, :], iota_row[:, 0:HG], part_f2[:, 1:2], None, ALU.is_equal)
            v.tensor_scalar(den_mask[:, :], iota_row[:, 0:HG], part_f2[:, 2:3], None, ALU.is_equal)
            v.tensor_scalar(state_mask[:, :], col_head[:, :, :].rearrange("p g c -> p (g c)"), part_f2[:, 0:1],
                            SCALE, ALU.is_equal, ALU.mult)
            order()
            for h in range(2):
                v.tensor_copy(vx[h][:, :, :, NUM:GW].rearrange("p c g n -> p (c g) n"),
                              den_mask[:, :].unsqueeze(1).broadcast_to([P, CPH * GROUPS, HG]))
            dve.wait_ge(setup_act, 1)
            v.tensor_scalar(silu_tmp[:, :], silu_tmp[:, :], 1.0, None, ALU.add)
            order()
            v.reciprocal(silu[:, :], silu_tmp[:, :])
            order()
            v.tensor_tensor(silu[:, :], silu[:, :], c_t[:, :], ALU.mult)
            order()
            v.tensor_copy(silu_bc[:, :, :], silu[:, :].unsqueeze(2).broadcast_to([P, B, P])).then_inc(setup_dve, 1)
            dve.wait_ge(setup_pe, 2)
            v.tensor_copy(col_sa[:, :], ps[:, 4, 0:B])
            v.tensor_scalar(col_ca1[:, :], ps[:, 4, B:2 * B], 1.0, None, ALU.add)
            v.tensor_copy(row_mod[:, :, :, :].rearrange("p b m e -> p b (m e)"), ps[:, 5:7, :])
            order()
            v.memset(den[0][:, :], 0.0).then_inc(consts, 1)
            v.tensor_scalar(row_cb1[:, :, :], row_mod[:, :, 2, :], 1.0, None, ALU.add)
            gate_raw = row_mod[:, :, 0:4:3, :]
            for b in range(B):
                v.scalar_tensor_tensor(gate_abs[:, b, :, :], gate_raw[:, b, :, :], -1.0, gate_raw[:, b, :, :],
                                       ALU.mult, ALU.max)
                v.tensor_scalar(gate_sgn[:, b, :, :], gate_raw[:, b, :, :], 0.0, 2.0, ALU.is_ge, ALU.mult)
            order()
            v.tensor_scalar(gate_abs[:, :, :, :], gate_abs[:, :, :, :], 0.25, None, ALU.max)
            v.tensor_scalar(gate_sgn[:, :, :, :], gate_sgn[:, :, :, :], -1.0, None, ALU.add)
            order()
            v.tensor_tensor(gates[:, :, :, :], gate_abs[:, :, :, :], gate_sgn[:, :, :, :], ALU.mult)
            order()
            v.tensor_scalar(gates[:, :, 1, :], gates[:, :, 1, :], 0.5, None, ALU.mult)
            v.tensor_tensor(wo_g[:, :, :], gates[:, :, 0, :], wo_t[:, :].unsqueeze(1).broadcast_to([P, B, E]), ALU.mult)
            order()
            dve.wait_ge(b2_ready, 1)

            def mask_attention(s, r):
                dve.wait_ge(pe_qk, GROUPS * s + r + 1)
                if s and r == 0:
                    dve.wait_ge(pe_o, HALF * s)
                v.tensor_tensor(attn[s % 2][:, r, :, :], ps[:, r % 2, :].rearrange("p (c l) -> p c l", l=CHUNK),
                                causal[:, :].unsqueeze(1).broadcast_to([P, CPH, CHUNK]),
                                ALU.mult).then_inc(dve_at, 1)

            def mask_sums(s, j):
                h = s % 2
                dve.wait_ge(pe_ds, HALF * s + j + 1)
                v.tensor_tensor(part[h][:, j, :, :].rearrange("p (a c) o -> p a c o", a=2),
                                ps[:, 4:6, 0:2 * OW].rearrange("p a (c o) -> p a c o", c=2),
                                state_mask[:, :].unsqueeze(1).unsqueeze(1).broadcast_to([P, 2, 2, OW]),
                                ALU.mult).then_inc(dve_sm, 1)
                order()
                before_tile = state[h][:, j, :] if (j or s % HALVES == 0) else state[1 - h][:, HALF, :]
                v.tensor_tensor(state[h][:, j + 1, :], before_tile, part[h][:, j, CPT - 1, :],
                                ALU.add).then_inc(dve_st, 1)

            def divide(s, j):
                o_ps = ps[:, 6 + j % 2, 0:OW].rearrange("p (g c) -> p g c", g=GROUPS)
                dve.wait_ge(pe_o, HALF * s + j + 1)
                v.tensor_scalar(den[j % 2][:, :].rearrange("p (g k) -> p g k", g=GROUPS), o_ps[:, :, NUM:GW],
                                1e-6, None, ALU.max)
                order()
                v.reciprocal(rden[j % 2][:, :], den[j % 2][:, :])
                order()
                v.tensor_tensor(
                    heads_out[s % 2][:, j, :].rearrange("p (g k d) -> p g k d", g=GROUPS, k=HG),
                    o_ps[:, :, 0:NUM].rearrange("p g (k d) -> p g k d", k=HG),
                    rden[j % 2][:, :].rearrange("p (g k) -> p g k", g=GROUPS).unsqueeze(3)
                    .broadcast_to([P, GROUPS, HG, D]), ALU.mult).then_inc(dve_ao, 1)

            def expert_of(s):
                h2 = rows[s % 2][:, :, 1, :]
                dve.wait_ge(pool_h2, s + 1)
                v.tensor_tensor(rt_s[:, :], h2[:, :, 0], h2[:, :, 1], ALU.add)
                order()
                v.scalar_tensor_tensor(rt_t[:, :], rt_s[:, :], -1.0, rt_s[:, :], ALU.mult, ALU.max)
                order()
                v.tensor_copy(rt_i[:, :], rt_t[:, :])
                v.tensor_scalar(rt_g[:, :], rt_s[:, :], 0.0, 2.0, ALU.is_ge, ALU.mult)
                order()
                v.tensor_copy(rt_f[:, :], rt_i[:, :])
                order()
                v.tensor_tensor(rt_m[:, :], rt_f[:, :], rt_t[:, :], ALU.is_gt)
                order()
                v.tensor_tensor(rt_f[:, :], rt_f[:, :], rt_m[:, :], ALU.subtract)
                order()
                v.scalar_tensor_tensor(rt_i[:, :], rt_g[:, :], -1.0, rt_f[:, :], ALU.add, ALU.mult)
                order()
                v.tensor_scalar(rt_i2[:, :], rt_i[:, :], EXPERTS - 1, None, ALU.bitwise_and)
                order()
                v.tensor_copy(rt_g[:, :], rt_i2[:, :])
                order()
                v.tensor_tensor(onehot[:, :, :], iota_row[:, 0:EXPERTS].unsqueeze(1).broadcast_to([P, HALF, EXPERTS]),
                                rt_g[:, :].unsqueeze(2).broadcast_to([P, HALF, EXPERTS]), ALU.is_equal)
                order()
                for j in range(HALF):
                    last = v.tensor_tensor(earlier[:, j + 1, :], earlier[:, j, :], onehot[:, j, :], ALU.add)
                    if j < HALF - 1:
                        order()
                last.then_inc(dve_oh, 1)

            def place_of(s):
                dve.wait_ge(pe_rank, s + 1)
                v.tensor_copy(earlier[:, 0, :], earlier[:, HALF, :])
                v.tensor_tensor(rank8[:, :, :], ps[:, 6, 0:HALF * EXPERTS].rearrange("p (t e) -> p t e", e=EXPERTS),
                                onehot[:, :, :], ALU.mult)
                order()
                v.tensor_reduce(rt_r[:, :], rank8[:, :, :], axis=AX.X, op=ALU.add)
                order()
                v.tensor_copy(rt_i[:, :], rt_r[:, :])
                order()
                v.tensor_scalar(rt_i2[:, :], rt_i[:, :], P - 1, None, ALU.bitwise_and)
                v.tensor_scalar(rt_i3[:, :], rt_i[:, :], 7, None, ALU.logical_shift_right)
                order()
                v.tensor_copy(rt_r[:, :], rt_i2[:, :])
                v.tensor_copy(rt_k[:, :], rt_i3[:, :])
                order()
                v.scalar_tensor_tensor(rt_k[:, :], rt_g[:, :], float(PLACES), rt_k[:, :], ALU.mult, ALU.add)
                v.tensor_tensor(oh_place[:, :, :], iota_row[:, :].unsqueeze(1).broadcast_to([P, HALF, P]),
                                rt_r[:, :].unsqueeze(2).broadcast_to([P, HALF, P]), ALU.is_equal)
                order()
                for j in range(HALF):
                    t = s * HALF + j
                    last = v.tensor_scalar(oh_token[:, j, :], iota_row[:, :], rt_k[:, j:j + 1],
                                           token1[:, t:t + 1], ALU.is_equal, ALU.mult)
                last.then_inc(dve_v, 1)

            def add_table(s):
                dve.wait_ge(pe_perm, s + 1)
                v.tensor_tensor(table[:, :], table[:, :], ps[:, 7, 0:P], ALU.add).then_inc(dve_perm, 1)

            for u in TURNS:
                has_a, has_b, has_c = parts_of(u)
                s, h = u + 1, (u + 1) % 2
                if has_b:
                    mask_attention(u, 0)
                    mask_sums(u, 0)
                if has_c:
                    c, hc = u - 1, (u - 1) % 2
                    dve.wait_ge(pe_y, c + 1)
                    if c >= 2:
                        dve.wait_ge(rows_out, 16 * (c - 1))
                    v.tensor_tensor(rows[hc][:, :, 0, :], ps[:, 7, :].rearrange("p (t e) -> p t e", e=E),
                                    x_all[:, c * HALF:(c + 1) * HALF, :], ALU.add).then_inc(dve_x1, 1)
                    order()
                    if c:
                        dve.wait_ge(pool_h2, c)
                    norm(lambda j: rows[hc][:, j, 0, :], xn2[hc]).then_inc(dve_xn2, 1)
                if has_b:
                    mask_attention(u, 1)
                if has_a:
                    dve.wait_ge(pool_eq, s + 1)
                    v.scalar_tensor_tensor(q_t[h][:, :], ps[:, 3, :], 0.0, e_q[h][:, :], ALU.max,
                                           ALU.add).then_inc(dve_q, 1)
                    dve.wait_ge(pool_ek, s + 1)
                    v.scalar_tensor_tensor(k_t[h][:, :], ps[:, 2, :], 0.0, e_k[h][:, :], ALU.max,
                                           ALU.add).then_inc(dve_k, 1)
                if has_b:
                    mask_sums(u, 1)
                    mask_attention(u, 2)
                for n in range(2):
                    if has_a:
                        dve.wait_ge(pool_ekt, 2 * s + n + 1)
                        dve.wait_ge(act_vt, 2 * s + n + 1)
                        kv = ps[:, 2 + n, :].rearrange("p (t c) -> p t c", t=2)
                        v.scalar_tensor_tensor(k_tok[h][:, 2 * n:2 * n + 2, :], kv[:, :, 0:P], 0.0,
                                               e_kt[h][:, 2 * n:2 * n + 2, :], ALU.max, ALU.add).then_inc(dve_kt, 1)
                    if has_b and n == 0:
                        mask_sums(u, 2)
                if has_c:
                    expert_of(u - 1)
                if has_a:
                    dve.wait_ge(act_qhi, s + 1)
                    v.tensor_tensor(q_lo[h][:, :], q_t[h][:, :], q_hi[h][:, :], ALU.subtract).then_inc(dve_qlo, 1)
                    dve.wait_ge(act_khi, s + 1)
                    v.tensor_tensor(k_lo[h][:, :], k_t[h][:, :], k_hi[h][:, :], ALU.subtract).then_inc(dve_klo, 1)
                    for k in range(HG):
                        last = v.tensor_scalar(kx_hi[h][:, :, k, :], k_hi[h][:, :].rearrange("p (c m) -> p c m", m=CHUNK),
                                               head_mask[:, k:k + 1], None, ALU.mult)
                    last.then_inc(dve_kx, 1)
                if has_b:
                    mask_attention(u, 3)
                    mask_sums(u, 3)
                if has_c:
                    place_of(u - 1)
                    add_table(u - 1)
                if has_b:
                    for j in range(HALF):
                        divide(u, j)
                if u + 2 < STEPS:
                    if u < 0:
                        dve.wait_ge(in_x, 16)
                    norm_x(u + 2)

            order()
            v.tensor_copy(table16[:, :], table[:, :]).then_inc(dve_run, 1)
            dve.wait_ge(pe_total, 1)
            v.tensor_scalar(total[:, :], ps[:, 7, 0:EXPERTS], float(P - 1), None, ALU.add)
            order()
            v.tensor_copy(tot_i[:, :], total[:, :])
            order()
            v.tensor_scalar(tot_i[:, :], tot_i[:, :], 7, None, ALU.logical_shift_right)
            order()
            v.tensor_copy(tiles_of[:, :], tot_i[:, :])
            order()
            v.tensor_copy(ends[:, 0:1], tiles_of[:, 0:1])
            order()
            for e in range(1, EXPERTS):
                v.tensor_tensor(ends[:, e:e + 1], ends[:, e - 1:e], tiles_of[:, e:e + 1], ALU.add)
                order()
            all_s = [P, SLOTS, EXPERTS]
            v.tensor_tensor(passed[:, :, :], ends[:, :].unsqueeze(1).broadcast_to(all_s),
                            iota_row[:, 0:SLOTS].unsqueeze(2).broadcast_to(all_s), ALU.is_le)
            order()
            v.tensor_tensor(weighed[:, :, :], passed[:, :, :], tiles_of[:, :].unsqueeze(1).broadcast_to(all_s), ALU.mult)
            v.tensor_reduce(slot_g[:, :], passed[:, :, :], axis=AX.X, op=ALU.add)
            order()
            v.tensor_reduce(slot_b[:, :], weighed[:, :, :], axis=AX.X, op=ALU.add)
            v.tensor_copy(slot_gi[:, :], slot_g[:, :])
            order()
            v.tensor_tensor(slot_c[:, :], iota_row[:, 0:SLOTS], slot_b[:, :], ALU.subtract)
            v.tensor_scalar(slot_gm[:, :], slot_gi[:, :], EXPERTS - 1, None, ALU.bitwise_and)
            order()
            v.scalar_tensor_tensor(slot_c[:, :], slot_g[:, :], float(PLACES), slot_c[:, :], ALU.mult, ALU.add)
            order()
            v.tensor_scalar(pick[:, :], slot_c[:, :], part_f[:, 0:1], None, ALU.is_equal).then_inc(dve_pick, 1)
            dve.wait_ge(pe_slots, 1)
            v.tensor_copy(tok_f[:, :], ps[:, 6, 0:SLOTS])
            order()
            v.tensor_scalar(tok_e[:, :], tok_f[:, :], 0.5, part_far[:, 0:1], ALU.is_lt, ALU.mult)
            v.tensor_scalar(src_f[:, :], tok_f[:, :], -1.0, 0.0, ALU.add, ALU.max)
            v.tensor_scalar(second[:, :], tok_f[:, :], L + 0.5, None, ALU.is_gt)
            v.tensor_scalar(first[:, :], tok_f[:, :], L + 0.5, None, ALU.is_lt)
            order()
            v.tensor_copy(src_i[:, :], src_f[:, :])
            v.tensor_tensor(dst_f[:, :], tok_e[:, :], src_f[:, :], ALU.add)
            order()
            v.tensor_copy(dst_i[:, :], dst_f[:, :]).then_inc(dve_slots, 1)
            order()

            v.memset(den[0][:, :], 0.0).then_inc(y_free, 2)

            def relu_second(n, k):
                dve.wait_ge(act_w1, n + 1)
                dve.wait_ge(pe_w1, n * 2 + 2)
                for c in range(FC):
                    last = v.tensor_scalar(hid[k][:, 1, c, :], ps[:, 2 * k + 1, c * P:(c + 1) * P],
                                           b1_now[:, bass.ds(n, 1), FC + c], 0.0, ALU.add, ALU.max)
                last.then_inc(dve_hid, 1)

            def gate_of(n):
                v.tensor_scalar(gate_a[:, :], gates[:, 1, 1, :], second[:, bass.ds(n, 1)], None, ALU.mult)
                order()
                v.scalar_tensor_tensor(gate_b[:, :], gates[:, 0, 1, :], first[:, bass.ds(n, 1)], gate_a[:, :],
                                       ALU.mult, ALU.add)

            def finish(n, k):
                dve.wait_ge(pe_y2, n + 1)
                v.tensor_tensor(y_b[:, :], ps[:, 4 + k, 0:E], b2_now[:, bass.ds(n, 1), :].rearrange("p a e -> p (a e)"),
                                ALU.add).then_inc(y_free, 1)
                order()
                v.tensor_tensor(y_g[:, :], y_b[:, :], gate_b[:, :], ALU.mult)
                order()
                x1 = got[:, bass.ds(n, 1), 0, :].rearrange("p a e -> p (a e)")
                v.tensor_tensor(x1, y_g[:, :], x1, ALU.add).then_inc(dve_done, 1)

            relu_second(0, 0)
            with dve.Fori(0, SLOTS // 2) as i:
                for k in range(2):
                    gate_of(i * 2 + k)
                    relu_second(i * 2 + (k + 1), 1 - k)
                    finish(i * 2 + k, k)
            gate_of(SLOTS - 1)
            finish(SLOTS - 1, 0)

        @block.tensor
        def _(pe):
            def mm(out, lhsT, rhs, start=True, stop=True, **k):
                return nc.tensor.matmul(out, lhsT, rhs, start=start, stop=stop, **k)

            def tr(out, src, n=P):
                return nc.tensor.transpose(out, src, ident[0:n, 0:n])

            pe.wait_ge(const, 1)
            pe.wait_ge(in_small, 80)
            tr(ps[:, 0, 0:B], c_rows[0:B, :], B)
            for k in range(3):
                tr(ps[:, 1, k * P:(k + 1) * P], wqkv[:, k, :])
            tr(ps[:, 2, 0:P], wout[:, :])
            tr(ps[:, 3, 0:EXPERTS * FC], b1_rows[0:EXPERTS * FC, :], EXPERTS * FC).then_inc(setup_pe, 1)
            pe.wait_ge(setup_dve, 1)
            for k in range(2):
                mm(ps[:, 4, k * B:(k + 1) * B], wmod[:, k * E:(k + 1) * E], silu[:, :])
            for b in range(B):
                last = mm(ps[:, 5 + b, :], silu_bc[:, b, :], wmod[:, 2 * E:])
            last.then_inc(setup_pe, 1)
            pe.wait_ge(consts, 1)

            def chunk_attention(s, r):
                h, i = s % 2, GROUPS * s + r
                if r == 0:
                    pe.wait_ge(dve_qlo, s + 1)
                    pe.wait_ge(dve_kx, s + 1)
                    pe.wait_ge(act_kx, s + 1)
                if i >= 2:
                    pe.wait_ge(dve_at, i - 1)
                rp = slice(r * CHUNK, (r + 1) * CHUNK)
                for c in range(CPH):
                    o = ps[:, r % 2, c * CHUNK:(c + 1) * CHUNK]
                    cs = slice(c * CHUNK, (c + 1) * CHUNK)
                    hi = kx_hi[h][rp, c, :, :].rearrange("p k m -> p (k m)")
                    lo = kx_lo[h][rp, c, :, :].rearrange("p k m -> p (k m)")
                    mm(o, hi, q_hi[h][rp, cs], stop=False)
                    mm(o, hi, q_lo[h][rp, cs], start=False, stop=False)
                    last = mm(o, lo, q_hi[h][rp, cs], start=False)
                last.then_inc(pe_qk, 1)

            def chunk_sums(s, j):
                h = s % 2
                if j == 0:
                    pe.wait_ge(dve_kt, 2 * s + 2)
                if HALF * s + j:
                    pe.wait_ge(dve_sm, HALF * s + j)
                for c in range(CPT):
                    n = (c + 1) * CHUNK
                    last = mm(ps[:, 4 + c // 2, (c % 2) * OW:(c % 2 + 1) * OW], k_tok[h][0:n, j, :],
                              v_tok[h][0:n, j, :, :].rearrange("p g c -> p (g c)"))
                last.then_inc(pe_ds, 1)

            def outputs(s, j):
                h, bank = s % 2, 6 + j % 2
                if j == 0:
                    pe.wait_ge(act_vx, CPT * (s + 1))
                    pe.wait_ge(dve_at, GROUPS * (s + 1))
                pe.wait_ge(dve_st, HALF * s + j + 1)
                if j >= 2:
                    pe.wait_ge(dve_ao, HALF * s + j - 1)
                elif s:
                    pe.wait_ge((dve_v, dve_perm)[j], s)
                at_start = state[h][:, j, :] if (j or s % HALVES == 0) else state[1 - h][:, HALF, :]
                mm(ps[:, bank, 0:OW], q_t[h][:, j * P:(j + 1) * P], at_start, stop=False, skip_group_check=True)
                for c in range(1, CPT):
                    t = j * P + c * CHUNK
                    mm(ps[c * CHUNK:(c + 1) * CHUNK, bank, 0:OW], q_t[h][:, t:t + CHUNK],
                       part[h][:, j, c - 1, :], start=False, stop=False, skip_group_check=True)
                for c in range(CPT):
                    for r in range(GROUPS):
                        last = mm(ps[c * CHUNK:(c + 1) * CHUNK, bank, r * GW:(r + 1) * GW],
                                  attn[h][:, r, j * CPT + c, :], vx[h][:, j * CPT + c, r, :],
                                  start=False, stop=True, skip_group_check=True)
                last.then_inc(pe_o, 1)

            for u in TURNS:
                has_a, has_b, has_c = parts_of(u)
                s, h = u + 1, (u + 1) % 2
                c, hc = u - 1, (u - 1) % 2
                if has_c:
                    pe.wait_ge(dve_ao, HALF * (c + 1))
                    for j in range(HALF):
                        last = tr(ps[:, 6, j * P:(j + 1) * P], heads_out[hc][:, j, :])
                    last.then_inc(pe_aT, 1)
                if has_b:
                    chunk_attention(u, 0)
                if has_c:
                    pe.wait_ge(act_aT, c + 1)
                    for j in range(HALF):
                        last = mm(ps[:, 7, j * P:(j + 1) * P], a_t[hc][:, j * P:(j + 1) * P], wo_g[:, c // HALVES, :])
                    last.then_inc(pe_y, 1)
                if has_b:
                    chunk_sums(u, 0)
                if has_a:
                    pe.wait_ge(dve_xn, s + 1)
                    if s:
                        pe.wait_ge(act_vx, CPT * s - 1)
                    for j in range(HALF):
                        last = tr(ps[:, 2, j * P:(j + 1) * P], xn[h][:, j, :])
                    last.then_inc(pe_xT, 1)
                if has_b:
                    chunk_attention(u, 1)
                if has_a:
                    pe.wait_ge(act_h, s + 1)
                    if s:
                        pe.wait_ge(act_vx, CPT * s)
                    mm(ps[:, 3, :], w_t[:, 0:E], h_t[h][:, :]).then_inc(pe_q, 1)
                    mm(ps[:, 2, :], w_t[:, E:2 * E], h_t[h][:, :]).then_inc(pe_k, 1)
                if has_b:
                    chunk_sums(u, 1)
                    chunk_attention(u, 2)
                if has_a:
                    pe.wait_ge(dve_q, s + 1)
                    mm(ps[:, 3, :], w_t[:, 2 * E:], h_t[h][:, :]).then_inc(pe_vT, 1)
                    for j in range(HALF):
                        if j == 0:
                            pe.wait_ge(dve_k, s + 1)
                        if j == 2:
                            pe.wait_ge(act_vTx, s + 1)
                        last = mm(ps[:, 2 + j // 2, (j % 2) * 256:(j % 2) * 256 + 256], h_t[h][:, j * P:(j + 1) * P],
                                  w_t[:, E:])
                        if j % 2:
                            last.then_inc(pe_kv, 1)
                if has_b:
                    chunk_sums(u, 2)
                if has_a:
                    for f in range(2):
                        pe.wait_ge(dve_kt, 2 * s + f + 1)
                        for i in range(4):
                            last = tr(ps[:, 2 + f % 2, i * P:(i + 1) * P],
                                      vx_t[h][:, 4 * f + i, :, :].rearrange("p k m -> p (k m)"))
                        last.then_inc(pe_vx, 1)
                if has_c:
                    pe.wait_ge(dve_oh, c + 1)
                    mm(ps[:, 6, 0:HALF * EXPERTS], before[:, :], onehot[:, :, :].rearrange("p t e -> p (t e)"), stop=False)
                    mm(ps[:, 6, 0:HALF * EXPERTS], ones[:, :], earlier[:, 0:HALF, :].rearrange("p t e -> p (t e)"),
                       start=False).then_inc(pe_rank, 1)
                if has_b:
                    chunk_attention(u, 3)
                    chunk_sums(u, 3)
                if has_a:
                    for f in range(2, CPH // 4):
                        pe.wait_ge(act_vx, s * CPT + f - 1)
                        for i in range(4):
                            last = tr(ps[:, 2 + f % 2, i * P:(i + 1) * P],
                                      vx_t[h][:, 4 * f + i, :, :].rearrange("p k m -> p (k m)"))
                        last.then_inc(pe_vx, 1)
                if has_c:
                    pe.wait_ge(dve_v, c + 1)
                    for j in range(HALF):
                        last = mm(ps[:, 7, 0:P], oh_token[:, j, :], oh_place[:, j, :], start=(j == 0), stop=(j == HALF - 1))
                    last.then_inc(pe_perm, 1)
                if has_b:
                    for j in range(HALF):
                        outputs(u, j)

            pe.wait_ge(dve_run, 1)
            mm(ps[:, 7, 0:EXPERTS], ones[:, :], earlier[:, 0, :]).then_inc(pe_total, 1)
            pe.wait_ge(dve_pick, 1)
            mm(ps[:, 6, 0:SLOTS], table16[:, :], pick[:, :]).then_inc(pe_slots, 1)

            def row_transposed(k):
                tr(ps[:, 6 + k, 0:P], h_row[k][:, :]).then_inc(pe_hT, 1)

            def hidden(k):
                for x in range(2):
                    for c in range(FC):
                        last = mm(ps[:, 2 * k + x, c * P:(c + 1) * P], w1_now[k][:, x, c * P:(c + 1) * P], h_col[k][:, :])
                    last.then_inc(pe_w1, 1)

            def second_layer(k, x, expert):
                for c in range(FC):
                    last = mm(ps[:, 4 + k, 0:E], hid[k][:, x, c, :],
                              w2[:, bass.ds(expert + x, 1), c, :].rearrange("p a e -> p (a e)"),
                              start=(x == 0 and c == 0), stop=(x == 1 and c == FC - 1))
                return last

            pe.wait_ge(in_w2, 16 * (EXPERTS + 1))
            pe.wait_ge(dve_slots, 1)
            for k in range(2):
                pe.wait_ge(act_row, k + 1)
                row_transposed(k)
            pe.wait_ge(act_hT, 1)
            pe.wait_ge(act_w1, 1)
            hidden(0)

            def slot(n, k):
                expert = pe.value_load(slot_gm[0:1, bass.ds(n, 1)], min_val=0, max_val=EXPERTS - 1)
                pe.wait_ge(act_row, n + 3)
                row_transposed(k)
                pe.wait_ge(act_hT, n + 2)
                pe.wait_ge(act_w1, n + 2)
                hidden(1 - k)
                pe.wait_ge(y_free, n + 1)
                pe.wait_ge(act_hid, n + 1)
                second_layer(k, 0, expert)
                pe.wait_ge(dve_hid, n + 1)
                second_layer(k, 1, expert).then_inc(pe_y2, 1)

            with pe.Fori(0, SLOTS // 2 - 1) as i:
                slot(i * 2, 0)
                slot(i * 2 + 1, 1)
            for n in range(SLOTS - SLOTS % 2 - 2, SLOTS):
                k = n % 2
                expert = pe.value_load(slot_gm[0:1, n:n + 1], min_val=0, max_val=EXPERTS - 1)
                if n + 2 < SLOTS:
                    pe.wait_ge(act_row, n + 3)
                    row_transposed(k)
                if n + 1 < SLOTS:
                    pe.wait_ge(act_hT, n + 2)
                    pe.wait_ge(act_w1, n + 2)
                    hidden(1 - k)
                pe.wait_ge(y_free, n + 1)
                pe.wait_ge(act_hid, n + 1)
                second_layer(k, 0, expert)
                pe.wait_ge(dve_hid, n + 1)
                second_layer(k, 1, expert).then_inc(pe_y2, 1)


_INS = ["L0_attn_x", "L0_attn_W_qkv", "L0_attn_W_out", "L0_ffn_W1", "L0_ffn_b1", "L0_ffn_W2", "L0_ffn_b2",
        "L0_c", "L0_wmod"]


def kernel(**inputs):
    import numpy as np
    import concourse.bacc as bacc
    from concourse.bass_utils import run_bass_kernel_spmd

    nc = bacc.Bacc("TRN2", target_bir_lowering=False, num_devices=1)
    arrays, aps = {}, []
    for name in _INS:
        a = np.ascontiguousarray(inputs[name])
        if name == "L0_attn_x":
            a = a.reshape(B * L, E)
        arrays[f"in_{name}"] = a
        aps.append(nc.dram_tensor(f"in_{name}", a.shape, mybir.dt.from_np(a.dtype), kind="ExternalInput").ap())
    out = nc.dram_tensor("out_rows", (B * L, E), F32, kind="ExternalOutput").ap()
    build(nc, *aps, out)
    r = run_bass_kernel_spmd(nc, [arrays], core_ids=[0])
    return r.results[0]["out_rows"].reshape(B, L, E)
```

```python
from contextlib import ExitStack

import concourse.bass as bass
from concourse import mybir

F32 = mybir.dt.float32
F16 = mybir.dt.float16
I32 = mybir.dt.int32
ALU = mybir.AluOpType
ACT = mybir.ActivationFunctionType
AX = mybir.AxisListType

P = 128
B, L, E = 2, 1024, 128
HEADS = 16
D = E // HEADS
CHUNK = 32
HALF = 4
HALVES = L // (P * HALF)
STEPS = B * HALVES
TILES = B * L // P
CPT = P // CHUNK
CPH = HALF * CPT
HG = P // CHUNK
GROUPS = HEADS // HG
GW = HG * D + HG
NUM = HG * D
OW = GROUPS * GW
EXPERTS = 8
FF = 512
FC = FF // P
SLOTS = TILES + EXPERTS - 1
PLACES = TILES
NO_PLACE = EXPERTS * PLACES
LN_EPS = 1e-5
SCALE = float(D) ** -0.5
RSQRT_SEED = float(0x5F3759DF)
W = HALF * P
SPREAD = 32.0


def build(nc, x_d, wqkv_d, wout_d, w1_d, b1_d, w2_d, b2_d, c_d, wmod_d, out_d):
    rows_d = nc.dram_tensor("rows_x1_h2", (B * L, 2 * E), F32, kind="Internal").ap()
    with ExitStack() as ctx:
        def sb(name, shape, dtype=F32):
            return ctx.enter_context(nc.sbuf_tensor(name, [P, *shape], dtype))

        def sem(name):
            return ctx.enter_context(nc.semaphore(name))

        ps = ctx.enter_context(nc.psum_tensor("ps", [P, 8, 512], F32))

        x_all = sb("x_all", [TILES, E])
        wqkv = sb("wqkv", [3, E])
        wout = sb("wout", [E])
        w_t = sb("w_t", [3 * E])
        wo_t = sb("wo_t", [E])
        wo_g = sb("wo_g", [B, E])
        wmod = sb("wmod", [6 * E])
        c_rows = sb("c_rows", [P])
        c_t = sb("c_t", [B])
        silu = sb("silu", [B])
        silu_tmp = sb("silu_tmp", [B])
        silu_bc = sb("silu_bc", [B, P])
        col_sa = sb("col_sa", [B])
        col_ca1 = sb("col_ca1", [B])
        row_mod = sb("row_mod", [B, 4, E])
        gates = sb("gates", [B, 2, E])
        row_cb1 = sb("row_cb1", [B, E])
        w1 = sb("w1", [EXPERTS + 1, FF])
        w2 = sb("w2", [EXPERTS + 1, FC, E])
        b1_rows = sb("b1_rows", [P])
        b1 = sb("b1", [(EXPERTS + 1) * FC])
        b2_pair = sb("b2_pair", [EXPERTS, E])

        ident = sb("ident", [P])
        before = sb("before", [P], F16)
        ones = sb("ones", [P], F16)
        causal = sb("causal", [CHUNK])
        iota_row = sb("iota_row", [P])
        part_i = sb("part_i", [1], I32)
        part_f = sb("part_f", [1])
        part_far = sb("part_far", [1])
        part_i2 = sb("part_i2", [3], I32)
        part_f2 = sb("part_f2", [3])
        token1 = sb("token1", [TILES])
        col_head = sb("col_head", [GROUPS, GW])
        state_mask = sb("state_mask", [OW])
        head_mask = sb("head_mask", [HG])
        den_mask = sb("den_mask", [HG])

        def two(name, shape, dtype=F32):
            return [sb(f"{name}{h}", shape, dtype) for h in range(2)]

        def one(name, shape, dtype=F32):
            return [sb(name, shape, dtype)] * 2

        stats = sb("stats", [TILES, 6])
        mean_var = sb("mean_var", [TILES, 2])
        rstd = sb("rstd", [TILES])
        stats2 = sb("stats2", [HALF, 6])
        mean_var2 = sb("mean_var2", [HALF, 2])
        rstd2 = sb("rstd2", [HALF])
        var = sb("var", [TILES])
        rs_a = sb("rs_a", [TILES])
        rs_b = sb("rs_b", [TILES])
        xn = two("xn", [HALF, E])
        part_a = sb("part_a", [5 * W + CPH * HG * CHUNK])
        h_t, e_q, e_k, k_t, e_kt_rows = [[part_a[:, k * W:(k + 1) * W]] * 2 for k in range(5)]
        e_kt = [e_kt_rows[0].rearrange("p (t e) -> p t e", e=P)] * 2
        vx_t = [part_a[:, 5 * W:].rearrange("p (c k m) -> p c k m", c=CPH, k=HG)] * 2
        w1_parts = part_a[:, 0:(EXPERTS + 1) * FF].bitcast(F16) \
            .rearrange("p (e a f) -> p e a f", e=EXPERTS + 1, a=2)
        arena = sb("arena", [SLOTS * 2 * E])
        q_t = [arena[:, h * W:(h + 1) * W] for h in range(2)]
        q_hi = two("q_hi", [W], F16)
        q_lo = two("q_lo", [W], F16)
        k_hi = one("k_hi", [W], F16)
        k_lo = one("k_lo", [W], F16)
        kx_all = sb("kx_all", [2, 2, CPH, HG, CHUNK], F16)
        kx_hi = [kx_all[:, 0, h, :, :, :] for h in range(2)]
        kx_lo = [kx_all[:, 1, h, :, :, :] for h in range(2)]
        k_tok = two("k_tok", [HALF, P])
        v_tok = two("v_tok", [HALF, GROUPS, GW])
        vx = [arena[:, 2 * W + h * CPH * OW:2 * W + (h + 1) * CPH * OW]
              .rearrange("p (c g n) -> p c g n", c=CPH, g=GROUPS) for h in range(2)]
        attn = one("attn", [GROUPS, CPH, CHUNK])
        flat = attn[0][:, :, :, :].rearrange("p g c l -> p (g c l)")
        part = one("part", [HALF, CPT, OW])
        b2 = part[0][:, :, :, :].rearrange("p t c o -> p (t c o)")[:, 0:(EXPERTS + 1) * E] \
            .rearrange("p (e d) -> p e d", d=E)
        state = two("state", [HALF + 1, OW])
        den = two("den", [HEADS])
        rden = two("rden", [HEADS])
        heads_out = one("heads_out", [HALF, E])
        a_t = one("a_t", [W])
        rows_all = sb("rows", [2, HALF, 2, E])
        rows = [rows_all[:, k, :, :, :] for k in range(2)]
        xn2 = sb("xn2", [HALF, E])
        gate_abs = xn2[:, :, :].rearrange("p (b k) e -> p b k e", b=B)
        gate_sgn = a_t[0][:, :].rearrange("p (b k e) -> p b k e", b=B, k=2)
        rt_s = two("rt_s", [2 * HALF])
        rt_t = two("rt_t", [2 * HALF])
        rt_i = two("rt_i", [2 * HALF], I32)
        rt_f = two("rt_f", [2 * HALF])
        rt_m = two("rt_m", [2 * HALF])
        rt_g = sb("rt_g", [TILES])
        rt_r = two("rt_r", [2 * HALF])
        rt_k = two("rt_k", [2 * HALF])
        rt_i2 = sb("rt_i2", [2 * HALF], I32)
        rt_i3 = sb("rt_i3", [2 * HALF], I32)
        onehot = sb("onehot", [TILES, EXPERTS], F16)
        earlier = sb("earlier", [STEPS - 1, EXPERTS], F16)
        rank_sb = sb("rank_sb", [HALF, EXPERTS])
        rank8 = two("rank8", [2 * HALF, EXPERTS])
        oh_place = two("oh_place", [2 * HALF, P], F16)
        oh_token = two("oh_token", [2 * HALF, P], F16)
        table = sb("table", [P])
        table16 = sb("table16", [P], F16)
        total = sb("total", [EXPERTS])
        tot_i = sb("tot_i", [EXPERTS], I32)
        tiles_of = sb("tiles_of", [EXPERTS])
        ends = two("ends", [EXPERTS])
        by_expert = sb("by_expert", [2, SLOTS, EXPERTS])
        passed, weighed = by_expert[:, 0, :, :], by_expert[:, 1, :, :]
        slot_gb = sb("slot_gb", [2, SLOTS])
        slot_g, slot_b = slot_gb[:, 0, :], slot_gb[:, 1, :]
        slot_c = sb("slot_c", [SLOTS])
        slot_gi = sb("slot_gi", [SLOTS], I32)
        slot_gm = sb("slot_gm", [SLOTS], I32)
        pick = sb("pick", [SLOTS], F16)
        tok_f = sb("tok_f", [SLOTS])
        tok_e = sb("tok_e", [SLOTS])
        src_f = sb("src_f", [SLOTS])
        src_i = sb("src_i", [SLOTS], I32)
        dst_f = sb("dst_f", [SLOTS])
        dst_i = sb("dst_i", [SLOTS], I32)
        second = sb("second", [SLOTS])
        first = sb("first", [SLOTS])
        got = arena[:, :].rearrange("p (n a e) -> p n a e", n=SLOTS, a=2)
        h_row = two("h_row", [E])
        h_hi = two("h_hi", [P], F16)
        h_lo = two("h_lo", [P], F16)
        w1_now = [flat[:, k * 2 * FF:(k + 1) * 2 * FF].bitcast(F16).rearrange("p (x a f) -> p x a f", x=2, a=2)
                  for k in range(2)]
        hid = [part[0][:, :, :, :].rearrange("p t c o -> p (t c o)")[:, k * 2 * FF:(k + 1) * 2 * FF]
               .rearrange("p (x c t) -> p x c t", x=2, c=FC) for k in range(2)]
        b2_now = kx_all[:, :, :, :, :, :].rearrange("p a h c k m -> p (a h c k m)").bitcast(F32)[:, 0:SLOTS * E] \
            .rearrange("p (n e) -> p n e", n=SLOTS)
        b1_now = sb("b1_now", [SLOTS, 2 * FC])
        y_b = two("y_b", [E])
        gate_a = two("gate_a", [E])
        gate_b = two("gate_b", [E])
        y_g = two("y_g", [E])
        done = got[:, :, 0, :]

        in_small = sem("in_small")
        in_x0 = sem("in_x0")
        in_x = sem("in_x")
        in_w1 = sem("in_w1")
        in_w2 = sem("in_w2")
        in_b2 = sem("in_b2")
        const = sem("const")
        masks = sem("masks")
        setup_pe = sem("setup_pe")
        setup_act = sem("setup_act")
        setup_dve = sem("setup_dve")
        dve_cols = sem("dve_cols")
        dve_gates = sem("dve_gates")
        dve_stats = sem("dve_stats")
        b2_ready = sem("b2_ready")
        dve_xn = sem("dve_xn")
        pool_xn = sem("pool_xn")
        pe_xT = sem("pe_xT")
        pe_q = sem("pe_q")
        pe_k = sem("pe_k")
        pe_vT = sem("pe_vT")
        pe_kv = sem("pe_kv")
        pe_vx = sem("pe_vx")
        pe_qk = sem("pe_qk")
        pe_ds = sem("pe_ds")
        pe_o = sem("pe_o")
        pe_aT = sem("pe_aT")
        pe_y = sem("pe_y")
        pe_rank = sem("pe_rank")
        pe_perm = sem("pe_perm")
        act_h = sem("act_h")
        act_eq = sem("act_eq")
        act_ek = sem("act_ek")
        act_vTx = sem("act_vTx")
        act_vt = sem("act_vt")
        act_qhi = sem("act_qhi")
        act_khi = sem("act_khi")
        act_kx = sem("act_kx")
        act_vx = sem("act_vx")
        act_aT = sem("act_aT")
        act_rank = sem("act_rank")
        dve_q = sem("dve_q")
        dve_k = sem("dve_k")
        dve_kt = sem("dve_kt")
        dve_qlo = sem("dve_qlo")
        dve_klo = sem("dve_klo")
        dve_kx = sem("dve_kx")
        dve_at = sem("dve_at")
        dve_sm = sem("dve_sm")
        dve_st = sem("dve_st")
        dve_ao = sem("dve_ao")
        dve_x1 = sem("dve_x1")
        dve_h2 = sem("dve_h2")
        dve_perm = sem("dve_perm")
        pool_oh = sem("pool_oh")
        pool_v = sem("pool_v")
        dve_oh = sem("dve_oh")
        dve_v = sem("dve_v")
        dve_run = sem("dve_run")
        pe_total = sem("pe_total")
        dve_passed = sem("dve_passed")
        pool_slots = sem("pool_slots")
        dve_pick = sem("dve_pick")
        pe_slots = sem("pe_slots")
        dve_src = sem("dve_src")
        dve_slots = sem("dve_slots")
        rows_out = sem("rows_out")
        gathered_even = sem("gathered_even")
        gathered_odd = sem("gathered_odd")
        gathered = (gathered_even, gathered_odd)
        dve_row = sem("dve_row")
        pe_hT = sem("pe_hT")
        act_hT = sem("act_hT")
        pool_w1 = sem("pool_w1")
        act_w1hi = sem("act_w1hi")
        pool_w1lo = sem("pool_w1lo")
        act_bias = sem("act_bias")
        dve_w1 = sem("dve_w1")
        dve_hlo = sem("dve_hlo")
        pe_w1 = sem("pe_w1")
        act_hid = sem("act_hid")
        act_hid2 = sem("act_hid2")
        dve_hid = sem("dve_hid")
        act_gate = sem("act_gate")
        pe_y2 = sem("pe_y2")
        y_free = sem("y_free")
        dve_gated = sem("dve_gated")
        gated_free = sem("gated_free")
        scattered = sem("scattered")
        turns = sem("turns")

        def wait_alone(eng, semaphore, value):
            eng.wait_ge(semaphore, value)
            eng.sem_inc(turns, 1)

        TURNS = range(-1, STEPS + 1)

        def parts_of(u):
            return u + 1 < STEPS, 0 <= u < STEPS, u > 0

        def banks_of(s):
            return (3, 2, 0, 1, 5) if s == 0 else (3, 2, 3, 2, 3)

        block = ctx.enter_context(nc.Block())

        @block.sync
        def _(sp):
            with nc.allow_non_contiguous_dma(reason="rows of experts"):
                sp.dma_start(x_all[:, 0:HALF, :], x_d[0:W, :].rearrange("(t p) e -> p t e", p=P)).then_inc(in_x0, 16)
                sp.dma_start(c_rows[0:B, :], c_d).then_inc(in_small, 16)
                sp.dma_start(wqkv[:, :, :], wqkv_d.rearrange("(g o) e -> o g e", o=P)).then_inc(in_small, 16)
                sp.dma_start(wmod[:, :], wmod_d).then_inc(in_small, 16)
                sp.dma_start(wout[:, :], wout_d).then_inc(in_small, 16)
                sp.dma_start(b1_rows[0:EXPERTS * FC, :], b1_d.rearrange("e (c p) -> (e c) p", p=P)).then_inc(in_small, 16)
                sp.dma_start(x_all[:, HALF:, :], x_d[W:, :].rearrange("(t p) e -> p t e", p=P)).then_inc(in_x, 16)
                sp.dma_start(b2[:, 0:EXPERTS, :], b2_d.rearrange("e d -> (e d)").partition_broadcast(P)
                             .rearrange("p (e d) -> p e d", d=E)).then_inc(in_b2, 16)
                sp.dma_start(b2[:, EXPERTS, :], b2_d[0, :].partition_broadcast(P)).then_inc(in_b2, 16)
                w1_v = w1_d.rearrange("e d f -> d e f")
                w2_v = w2_d.rearrange("e (c p) d -> p e c d", p=P)
                for e in range(EXPERTS):
                    sp.dma_start(w1[:, e, :], w1_v[:, e, :]).then_inc(in_w1, 16)
                    sp.dma_start(w2[:, e, :, :], w2_v[:, e, :, :]).then_inc(in_w2, 16)
                sp.dma_start(w1[:, EXPERTS, :], w1_v[:, 0, :]).then_inc(in_w1, 16)
                sp.dma_start(w2[:, EXPERTS, :, :], w2_v[:, 0, :, :]).then_inc(in_w2, 16)
                for s in range(STEPS):
                    sp.wait_ge(dve_h2, s + 1)
                    if s:
                        sp.wait_ge(rows_out, 16 * s)
                    sp.dma_start(rows_d[s * W:(s + 1) * W, :].rearrange("(t p) c -> p t c", p=P),
                                 rows[s % 2][:, :, :, :].rearrange("p t a e -> p t (a e)")).then_inc(rows_out, 16)
                sp.wait_ge(rows_out, 16 * STEPS)

        @block.gpsimd
        def _(pool):
            g = nc.gpsimd
            g.memset(ident[:, :], 0.0)
            g.memset(before[:, :], 1.0)
            g.memset(ones[:, :], 1.0)
            g.memset(causal[:, :], SCALE / SPREAD ** 2)
            imprecise = dict(allow_small_or_imprecise_dtypes=True)
            g.iota(iota_row[:, :], pattern=[[1, P]], base=0, channel_multiplier=0, **imprecise)
            g.iota(part_i[:, :], pattern=[[1, 1]], base=0, channel_multiplier=1)
            g.iota(part_f[:, :], pattern=[[1, 1]], base=0, channel_multiplier=1, **imprecise)
            g.iota(token1[:, :], pattern=[[P, TILES]], base=1, channel_multiplier=1, **imprecise)
            g.iota(col_head[:, :, 0:NUM].rearrange("p g (h d) -> p g h d", d=D),
                   pattern=[[HG, GROUPS], [1, HG], [0, D]], base=0, channel_multiplier=0, **imprecise)
            g.iota(col_head[:, :, NUM:GW], pattern=[[HG, GROUPS], [1, HG]], base=0, channel_multiplier=0,
                   **imprecise)
            pool.drain()
            g.affine_select(out=ident[:, :], in_=ident[:, :], compare_op=ALU.not_equal, fill=1.0, base=0,
                            pattern=[[-1, P]], channel_multiplier=1)
            g.affine_select(out=before[:, :], in_=before[:, :], compare_op=ALU.is_gt, fill=0.0, base=0,
                            pattern=[[1, P]], channel_multiplier=-1)
            for k in range(HG):
                pool.drain()
                rows_k = causal[k * CHUNK:(k + 1) * CHUNK, :]
                g.affine_select(out=rows_k, in_=rows_k, compare_op=ALU.is_ge, fill=0.0, base=0,
                                pattern=[[1, CHUNK]], channel_multiplier=-1)
            pool.drain()
            g.memset(state[0][:, 0, :], 0.0).then_inc(const, 1)
            pool.wait_ge(in_b2, 32)
            g.tensor_tensor(b2_pair[:, :, :], b2[:, 0:EXPERTS, :], b2[:, 1:EXPERTS + 1, :], ALU.add).then_inc(b2_ready, 1)

            def floor(y, f, i, m):
                g.tensor_copy(i, y)
                pool.drain()
                g.tensor_copy(f, i)
                pool.drain()
                g.tensor_tensor(m, f, y, ALU.subtract)
                pool.drain()
                g.tensor_scalar(m, m, 0.0, None, ALU.is_gt)
                pool.drain()
                g.tensor_tensor(f, f, m, ALU.subtract)
                pool.drain()

            def rest(x, f, divisor, out, m):
                g.tensor_scalar(m, f, -float(divisor), None, ALU.mult)
                pool.drain()
                g.tensor_tensor(out, x, m, ALU.add)
                pool.drain()

            def expert_of(c):
                h2 = rows[c % 2][:, :, 1, :]
                x, t, i, f, m = (buf[0][:, 0:HALF] for buf in (rt_s, rt_t, rt_i, rt_f, rt_m))
                k = rt_g[:, c * HALF:(c + 1) * HALF]
                g.tensor_tensor(x, h2[:, :, 0], h2[:, :, 1], ALU.add)
                pool.drain()
                g.tensor_scalar(k, x, 0.0, 2.0, ALU.is_ge, ALU.mult)
                pool.drain()
                g.tensor_scalar(k, k, -1.0, None, ALU.add)
                pool.drain()
                g.tensor_tensor(t, x, k, ALU.mult)
                pool.drain()
                floor(t, f, i, m)
                g.tensor_tensor(x, f, k, ALU.mult)
                pool.drain()
                g.tensor_scalar(t, x, 1.0 / EXPERTS, None, ALU.mult)
                pool.drain()
                floor(t, f, i, m)
                rest(x, f, EXPERTS, k, m)
                for j in range(HALF):
                    g.tensor_scalar(onehot[:, c * HALF + j, :], iota_row[:, 0:EXPERTS], k[:, j:j + 1], None, ALU.is_equal)
                pool.drain()
                for j in range(HALF):
                    last = g.tensor_tensor(earlier[:, c + 1, :], earlier[:, c if j == 0 else c + 1, :],
                                           onehot[:, c * HALF + j, :], ALU.add)
                    if j < HALF - 1:
                        pool.drain()
                return last

            def place_of(c):
                x, t, i, f, m, k = (buf[0][:, 0:HALF] for buf in (rt_r, rt_t, rt_i, rt_f, rt_m, rt_k))
                tiles, r8 = slice(c * HALF, (c + 1) * HALF), rank8[0][:, 0:HALF, :]
                g.tensor_tensor(r8, rank_sb[:, :, :], onehot[:, tiles, :], ALU.mult)
                pool.drain()
                for n in (EXPERTS // 2, EXPERTS // 4):
                    g.tensor_tensor(r8[:, :, 0:n], r8[:, :, 0:n], r8[:, :, n:2 * n], ALU.add)
                    pool.drain()
                g.tensor_tensor(x, r8[:, :, 0], r8[:, :, 1], ALU.add)
                pool.drain()
                g.tensor_scalar(t, x, 1.0 / P, None, ALU.mult)
                pool.drain()
                floor(t, f, i, m)
                rest(x, f, P, t, m)
                g.tensor_scalar(k, rt_g[:, tiles], float(PLACES), None, ALU.mult)
                pool.drain()
                g.tensor_tensor(k, k, f, ALU.add)
                pool.drain()
                for j in range(HALF):
                    tile = c * HALF + j
                    g.tensor_scalar(oh_place[0][:, j, :], iota_row[:, :], t[:, j:j + 1], None, ALU.is_equal)
                    last = g.tensor_scalar(oh_token[0][:, j, :], iota_row[:, :], k[:, j:j + 1],
                                           token1[:, tile:tile + 1], ALU.is_equal, ALU.mult)
                return last

            def norm_x(s):
                if s >= 2:
                    pool.wait_ge(pe_xT, s - 1)
                for j in range(HALF):
                    t = s * HALF + j
                    last = g.tensor_scalar(xn[s % 2][:, j, :], x_all[:, t, :], mean_var[:, t, 0:1], rstd[:, t:t + 1],
                                           ALU.subtract, ALU.mult)
                last.then_inc(pool_xn, 1)

            pool.wait_ge(in_x, 16)
            pool.wait_ge(dve_stats, 1)
            norm_x(1)
            norm_x(2)
            pool.wait_ge(in_w1, 16 * (EXPERTS + 1))
            g.tensor_scalar(w1[:, :, :], w1[:, :, :], SPREAD, None, ALU.mult).then_inc(pool_w1, 1)
            for c in range(STEPS - 2):
                pool.wait_ge(dve_h2, c + 1)
                expert_of(c).then_inc(pool_oh, 1)
                if c == 0:
                    norm_x(3)
            for c in range(STEPS - 2):
                pool.wait_ge(act_rank, c + 1)
                if c:
                    pool.wait_ge(pe_perm, c)
                place_of(c).then_inc(pool_v, 1)

            pool.wait_ge(act_w1hi, 1)
            g.tensor_tensor(w1_parts[:, :, 1, :], w1[:, :, :], w1_parts[:, :, 0, :], ALU.subtract).then_inc(pool_w1lo, 1)

            all_s = [P, SLOTS, EXPERTS]
            pool.wait_ge(dve_passed, 1)
            g.tensor_tensor(weighed, passed, tiles_of[:, :].unsqueeze(1).broadcast_to(all_s), ALU.mult)
            for n in (4, 2):
                pool.drain()
                g.tensor_tensor(by_expert[:, :, :, 0:n], by_expert[:, :, :, 0:n], by_expert[:, :, :, n:2 * n], ALU.add)
            pool.drain()
            g.tensor_tensor(slot_gb[:, :, :], by_expert[:, :, :, 0], by_expert[:, :, :, 1], ALU.add
                            ).then_inc(pool_slots, 1)

            pool.wait_ge(rows_out, 16 * STEPS)
            g.memset(rank_sb[:, :, :], 0.0).then_inc(gated_free, 2)
            pool.wait_ge(dve_src, 1)

            def gather(n):
                if n >= 2:
                    pool.wait_ge(gathered[n % 2], 16 * (n // 2))
                g.indirect_dma_start(out=got[:, n, :, :].rearrange("p a e -> p (a e)"), out_offset=None,
                                     in_=rows_d, in_offset=bass.IndirectOffsetOnAxis(ap=src_i[:, n:n + 1], axis=0)
                                     ).then_inc(gathered[n % 2], 16)

            ahead = 6
            for n in range(ahead):
                gather(n)
            pool.wait_ge(dve_slots, 1)
            for n in range(SLOTS):
                if n + ahead < SLOTS:
                    gather(n + ahead)
                pool.wait_ge(dve_gated, n + 1)
                g.tensor_tensor(done[:, n, :], y_g[n % 2][:, :], got[:, n, 0, :], ALU.add).then_inc(gated_free, 1)
                pool.wait_ge(gated_free, n + 3)
                g.indirect_dma_start(out=out_d, out_offset=bass.IndirectOffsetOnAxis(ap=dst_i[:, n:n + 1], axis=0),
                                     in_=done[:, n, :], in_offset=None, bounds_check=B * L - 1, oob_is_err=False
                                     ).then_inc(scattered, 16)
            pool.wait_ge(scattered, 16 * SLOTS)

        @block.scalar
        def _(act):
            a = nc.scalar
            act.wait_ge(setup_pe, 1)
            a.activation(silu_tmp[:, :], ps[:, 0, 0:B], ACT.Exp, scale=-1.0)
            a.activation(c_t[:, :], ps[:, 0, 0:B], ACT.Copy).then_inc(setup_act, 1)
            a.activation(w_t[:, :], ps[:, 1, 0:3 * E], ACT.Copy)
            a.activation(wo_t[:, :], ps[:, 2, 0:E], ACT.Copy)
            a.activation(b1[:, 0:EXPERTS * FC], ps[:, 3, 0:EXPERTS * FC], ACT.Copy, scale=SPREAD ** 2)
            a.activation(b1[:, EXPERTS * FC:], ps[:, 3, 0:FC], ACT.Copy, scale=SPREAD ** 2).then_inc(setup_act, 1)
            act.wait_ge(dve_cols, 1)

            def spread_values(s, f):
                act.wait_ge(pe_vx, s * CPT + f + 1)
                a.activation(vx[s % 2][:, 4 * f:4 * f + 4, :, 0:NUM].rearrange("p c g n -> p (c g) n"),
                             ps[:, 2 + f % 2, :].rearrange("p (c n) -> p c n", n=NUM), ACT.Copy).then_inc(act_vx, 1)

            def high_parts(s):
                act.wait_ge(dve_q, s + 1)
                a.activation(q_hi[s % 2][:, :], q_t[s % 2][:, :], ACT.Copy, scale=SPREAD).then_inc(act_qhi, 1)
                act.wait_ge(dve_k, s + 1)
                a.activation(k_hi[s % 2][:, :], k_t[s % 2][:, :], ACT.Copy, scale=SPREAD).then_inc(act_khi, 1)

            for u in TURNS:
                has_a, has_b, has_c = parts_of(u)
                s, h, b = u + 1, (u + 1) % 2, (u + 1) // HALVES
                c = u - 1
                if has_c and has_b:
                    act.wait_ge(pe_aT, c + 1)
                    if c == 0:
                        act.wait_ge(dve_gates, 1)
                    a.activation(a_t[0][:, :], ps[:, 6, :], ACT.Copy).then_inc(act_aT, 1)
                elif has_c:
                    for n in range(2):
                        act.wait_ge(pe_aT, c + 1 + n)
                        a.activation(a_t[0][:, n * 2 * P:(n + 1) * 2 * P], ps[:, 2 - 2 * n, 0:2 * P],
                                     ACT.Copy).then_inc(act_aT, 1)
                if has_a:
                    act.wait_ge(pe_xT, s + 1)
                    bank_q, bank_k, bank_v, *bank_kv = banks_of(s)
                    a.activation(h_t[h][:, :], ps[:, 2, :], ACT.Identity, scale=col_ca1[:, b:b + 1],
                                 bias=col_sa[:, b:b + 1]).then_inc(act_h, 1)
                    act.wait_ge(pe_q, s + 1)
                    if s:
                        act.wait_ge(dve_q, s)
                    a.activation(e_q[h][:, :], ps[:, bank_q, :], ACT.Exp)
                    a.activation(q_t[h][:, :], ps[:, bank_q, :], ACT.Relu).then_inc(act_eq, 1)
                    act.wait_ge(pe_k, s + 1)
                    if s:
                        act.wait_ge(dve_klo, s)
                    a.activation(e_k[h][:, :], ps[:, bank_k, :], ACT.Exp)
                    a.activation(k_t[h][:, :], ps[:, bank_k, :], ACT.Relu).then_inc(act_ek, 1)
                    if s == 0:
                        high_parts(s)
                    act.wait_ge(pe_vT, s + 1)
                    if s == 0:
                        act.wait_ge(masks, 1)
                    else:
                        act.wait_ge(pe_vx, s * CPT)
                    for k in range(HG):
                        last = a.activation(vx_t[h][:, :, k, :], ps[:, bank_v, :].rearrange("p (c m) -> p c m", m=CHUNK),
                                            ACT.Copy, scale=head_mask[:, k:k + 1])
                    last.then_inc(act_vTx, 1)
                    if s:
                        high_parts(s)
                    for n in range(2):
                        kv = ps[:, bank_kv[n], :].rearrange("p (t c) -> p t c", t=2)
                        two_tiles = slice(2 * n, 2 * n + 2)
                        act.wait_ge(pe_kv, 2 * s + n + 1)
                        if s:
                            act.wait_ge(dve_kt, 2 * s - 1 + n)
                        a.activation(e_kt[h][:, two_tiles, :], kv[:, :, 0:P], ACT.Exp)
                        a.activation(k_tok[h][:, two_tiles, :], kv[:, :, 0:P], ACT.Relu)
                        for t in range(2):
                            last = a.activation(v_tok[h][:, 2 * n + t, :, 0:NUM],
                                                kv[:, t, P:].rearrange("p (g c) -> p g c", g=GROUPS), ACT.Copy)
                        last.then_inc(act_vt, 1)
                if u == 3:
                    act.wait_ge(pool_w1, 1)
                    act.wait_ge(dve_kt, 2 * STEPS)
                    a.activation(w1_parts[:, :, 0, :], w1[:, :, :], ACT.Copy).then_inc(act_w1hi, 1)
                if u >= 2 and u - 2 < STEPS - 2:
                    act.wait_ge(pe_rank, u - 1)
                    if u > 2:
                        act.wait_ge(pool_v, u - 2)
                    a.activation(rank_sb[:, :, :].rearrange("p t e -> p (t e)"), ps[:, 6, 0:HALF * EXPERTS],
                                 ACT.Copy).then_inc(act_rank, 1)
                if has_a:
                    spread_values(s, 0)
                    spread_values(s, 1)
                    if s:
                        act.wait_ge(dve_klo, s + 1)
                        for k in range(HG):
                            last = a.activation(kx_lo[h][:, :, k, :],
                                                k_lo[h][:, :].rearrange("p (c m) -> p c m", m=CHUNK),
                                                ACT.Copy, scale=head_mask[:, k:k + 1])
                        last.then_inc(act_kx, 1)
                    spread_values(s, 2)
                    spread_values(s, 3)

            def stage_biases(n):
                expert = act.value_load(slot_gm[0:1, bass.ds(n, 1)], min_val=0, max_val=EXPERTS - 1)
                a.activation(b1_now[:, bass.ds(n, 1), :].rearrange("p a c -> p (a c)"),
                             b1[:, bass.ds(expert * FC, 2 * FC)], ACT.Copy)
                a.activation(b2_now[:, bass.ds(n, 1), :].rearrange("p a e -> p (a e)"),
                             b2_pair[:, bass.ds(expert, 1), :].rearrange("p a e -> p (a e)"), ACT.Copy).then_inc(act_bias, 1)

            def column(k):
                a.activation(h_hi[k][:, :], ps[:, 6 + k, 0:P], ACT.Copy, scale=SPREAD).then_inc(act_hT, 1)

            def relu_first(n, k):
                for c in range(FC):
                    last = a.activation(hid[k][:, 0, c, :], ps[:, 2 * k, c * P:(c + 1) * P], ACT.Relu,
                                        bias=b1_now[:, bass.ds(n, 1), c])
                last.then_inc(act_hid, 1)

            def relu_second(n):
                for c in range(FC):
                    last = a.activation(hid[0][:, 1, c, :], ps[:, 1, c * P:(c + 1) * P], ACT.Relu,
                                        bias=b1_now[:, bass.ds(n, 1), FC + c])
                last.then_inc(act_hid2, 1)

            def gate_second(n, k):
                act.wait_ge(y_free, n + 1)
                a.activation(gate_a[k][:, :], gates[:, 1, 1, :], ACT.Copy, scale=second[:, bass.ds(n, 1)]
                             ).then_inc(act_gate, 1)

            act.wait_ge(dve_slots, 1)
            act.wait_ge(b2_ready, 1)
            stage_biases(0)
            for n in range(2):
                act.wait_ge(pe_hT, n + 1)
                column(n)
            stage_biases(1)
            act.drain()
            with act.Fori(0, SLOTS // 2 - 1) as i:
                for k in range(2):
                    n = i * 2 + k
                    wait_alone(act, pe_w1, n * 2 + 1)
                    relu_first(n, k)
                    stage_biases(n + 2)
                    wait_alone(act, pe_w1, n * 2 + 2)
                    if k == 0:
                        relu_second(n)
                    wait_alone(act, pe_hT, n + 3)
                    column(k)
                    gate_second(n, k)
            for n in range(SLOTS - SLOTS % 2 - 2, SLOTS):
                k = n % 2
                act.wait_ge(pe_w1, 2 * n + 1)
                relu_first(n, k)
                act.wait_ge(pe_w1, 2 * n + 2)
                if k == 0:
                    relu_second(n)
                if n + 2 < SLOTS:
                    stage_biases(n + 2)
                    act.wait_ge(pe_hT, n + 3)
                    column(k)
                gate_second(n, k)

        @block.vector
        def _(dve):
            v = nc.vector
            order = dve.drain

            def statistics(src, stats_of, means):
                for j, x in enumerate(src):
                    v.bn_stats(out=stats_of[:, j, :], in_=x)
                order()
                for j in range(len(src)):
                    v.bn_aggr(out=means[:, j, :], in_=stats_of[:, j, :])
                order()

            def root_seed(means, r, x):
                v.tensor_scalar(x, means[:, :, 1], LN_EPS, None, ALU.add)
                order()
                v.tensor_scalar(r.bitcast(I32), x.bitcast(I32), -0.5, RSQRT_SEED, ALU.mult, ALU.add)
                order()

            def root_steps(r, x, steps):
                ra, rb = rs_a[:, 0:x.shape[1]], rs_b[:, 0:x.shape[1]]
                for _ in range(steps):
                    v.scalar_tensor_tensor(ra, r, -0.5, x, ALU.mult, ALU.mult)
                    order()
                    v.tensor_tensor(rb, ra, r, ALU.mult)
                    order()
                    v.scalar_tensor_tensor(r, rb, 1.5, r, ALU.add, ALU.mult)
                    order()

            dve.wait_ge(in_x0, 16)
            statistics([x_all[:, j, :] for j in range(HALF)], stats, mean_var)
            root_seed(mean_var[:, 0:HALF, :], rstd[:, 0:HALF], var[:, 0:HALF])
            root_steps(rstd[:, 0:HALF], var[:, 0:HALF], 3)
            dve.wait_ge(setup_act, 1)
            v.tensor_scalar(silu_tmp[:, :], silu_tmp[:, :], 1.0, None, ALU.add)
            order()
            v.reciprocal(silu[:, :], silu_tmp[:, :])
            order()
            v.tensor_tensor(silu[:, :], silu[:, :], c_t[:, :], ALU.mult).then_inc(setup_dve, 1)
            for j in range(HALF):
                last = v.tensor_scalar(xn[0][:, j, :], x_all[:, j, :], mean_var[:, j, 0:1], rstd[:, j:j + 1],
                                       ALU.subtract, ALU.mult)
            last.then_inc(dve_xn, 1)
            order()
            v.tensor_copy(silu_bc[:, :, :], silu[:, :].unsqueeze(2).broadcast_to([P, B, P])).then_inc(setup_dve, 1)
            dve.wait_ge(const, 1)
            v.tensor_scalar(part_i2[:, 0:1], part_i[:, :], 3, None, ALU.logical_shift_right)
            v.tensor_scalar(part_i2[:, 1:2], part_i[:, :], 3, HG - 1, ALU.logical_shift_right, ALU.bitwise_and)
            v.tensor_scalar(part_i2[:, 2:3], part_i[:, :], 5, None, ALU.logical_shift_right)
            dve.wait_ge(setup_pe, 2)
            v.tensor_copy(col_sa[:, :], ps[:, 4, 0:B])
            v.tensor_scalar(col_ca1[:, :], ps[:, 4, B:2 * B], 1.0, None, ALU.add).then_inc(dve_cols, 1)
            order()
            v.tensor_copy(part_f2[:, :], part_i2[:, :])
            v.tensor_scalar(part_far[:, :], part_f[:, :], float(2 * B * L), None, ALU.add)
            order()
            v.tensor_scalar(den_mask[:, :], iota_row[:, 0:HG], part_f2[:, 2:3], None, ALU.is_equal)
            v.tensor_scalar(state_mask[:, :], col_head[:, :, :].rearrange("p g c -> p (g c)"), part_f2[:, 0:1],
                            SCALE, ALU.is_equal, ALU.mult)
            v.tensor_scalar(head_mask[:, :], iota_row[:, 0:HG], part_f2[:, 1:2], None, ALU.is_equal).then_inc(masks, 1)
            order()
            v.memset(table[:, :], 0.0)
            v.memset(earlier[:, 0, :], 0.0)
            for h in range(2):
                v.memset(v_tok[h][:, :, :, NUM:GW], 1.0)
                v.tensor_copy(vx[h][:, :, :, NUM:GW].rearrange("p c g n -> p (c g) n"),
                              den_mask[:, :].unsqueeze(1).broadcast_to([P, CPH * GROUPS, HG]))

            dve.wait_ge(in_x, 16)
            statistics([x_all[:, t, :] for t in range(HALF, TILES)], stats[:, HALF:, :], mean_var[:, HALF:, :])

            def make_gates():
                gate_raw = row_mod[:, :, 0:4:3, :]
                dve.wait_ge(setup_pe, 3)
                v.tensor_copy(row_mod[:, :, :, :].rearrange("p b m e -> p b (m e)"), ps[:, 6:8, :])
                order()
                v.tensor_scalar(row_cb1[:, :, :], row_mod[:, :, 2, :], 1.0, None, ALU.add)
                for b in range(B):
                    v.scalar_tensor_tensor(gate_abs[:, b, :, :], gate_raw[:, b, :, :], -1.0, gate_raw[:, b, :, :],
                                           ALU.mult, ALU.max)
                    v.tensor_scalar(gate_sgn[:, b, :, :], gate_raw[:, b, :, :], 0.0, 2.0, ALU.is_ge, ALU.mult)
                order()
                v.tensor_scalar(gate_abs[:, :, :, :], gate_abs[:, :, :, :], 0.25, None, ALU.max)
                v.tensor_scalar(gate_sgn[:, :, :, :], gate_sgn[:, :, :, :], -1.0, None, ALU.add)
                order()
                v.tensor_tensor(gates[:, :, :, :], gate_abs[:, :, :, :], gate_sgn[:, :, :, :], ALU.mult)
                order()
                v.tensor_scalar(gates[:, :, 1, :], gates[:, :, 1, :], 0.5, None, ALU.mult)
                dve.wait_ge(setup_act, 2)
                v.tensor_tensor(wo_g[:, :, :], gates[:, :, 0, :], wo_t[:, :].unsqueeze(1).broadcast_to([P, B, E]),
                                ALU.mult).then_inc(dve_gates, 1)

            def mask_attention(s, r):
                dve.wait_ge(pe_qk, GROUPS * s + r + 1)
                if s and r == 0:
                    dve.wait_ge(pe_o, HALF * s)
                v.tensor_tensor(attn[s % 2][:, r, :, :], ps[:, r % 2, :].rearrange("p (c l) -> p c l", l=CHUNK),
                                causal[:, :].unsqueeze(1).broadcast_to([P, CPH, CHUNK]),
                                ALU.mult).then_inc(dve_at, 1)

            def mask_sums(s, j):
                h = s % 2
                dve.wait_ge(pe_ds, HALF * s + j + 1)
                v.tensor_tensor(part[h][:, j, :, :].rearrange("p (a c) o -> p a c o", a=2),
                                ps[:, 4:6, 0:2 * OW].rearrange("p a (c o) -> p a c o", c=2),
                                state_mask[:, :].unsqueeze(1).unsqueeze(1).broadcast_to([P, 2, 2, OW]),
                                ALU.mult).then_inc(dve_sm, 1)
                order()
                before_tile = state[h][:, j, :] if (j or s % HALVES == 0) else state[1 - h][:, HALF, :]
                v.tensor_tensor(state[h][:, j + 1, :], before_tile, part[h][:, j, CPT - 1, :],
                                ALU.add).then_inc(dve_st, 1)

            def divide(s, j):
                o_ps = ps[:, 6 + j % 2, 0:OW].rearrange("p (g c) -> p g c", g=GROUPS)
                dve.wait_ge(pe_o, HALF * s + j + 1)
                v.tensor_scalar(den[j % 2][:, :].rearrange("p (g k) -> p g k", g=GROUPS), o_ps[:, :, NUM:GW],
                                1e-6, None, ALU.max)
                order()
                v.reciprocal(rden[j % 2][:, :], den[j % 2][:, :])
                order()
                v.tensor_tensor(
                    heads_out[s % 2][:, j, :].rearrange("p (g k d) -> p g k d", g=GROUPS, k=HG),
                    o_ps[:, :, 0:NUM].rearrange("p g (k d) -> p g k d", k=HG),
                    rden[j % 2][:, :].rearrange("p (g k) -> p g k", g=GROUPS).unsqueeze(3)
                    .broadcast_to([P, GROUPS, HG, D]), ALU.mult).then_inc(dve_ao, 1)

            def scale_x1(c):
                for j in range(HALF):
                    v.scalar_tensor_tensor(xn2[:, j, :], rows[c % 2][:, j, 0, :], mean_var2[:, j, 0:1],
                                           row_cb1[:, c // HALVES, :], ALU.subtract, ALU.mult)

            def make_h2(c):
                for j in range(HALF):
                    last = v.scalar_tensor_tensor(rows[c % 2][:, j, 1, :], xn2[:, j, :], rstd2[:, j:j + 1],
                                                  row_mod[:, c // HALVES, 1, :], ALU.mult, ALU.add)
                last.then_inc(dve_h2, 1)

            for u in TURNS:
                has_a, has_b, has_c = parts_of(u)
                s, h = u + 1, (u + 1) % 2
                c, hc = u - 1, (u - 1) % 2
                late = u == STEPS - 1
                if has_b:
                    if u == 0:
                        dve.wait_ge(b2_ready, 1)
                    mask_attention(u, 0)
                    mask_sums(u, 0)
                if u == 0:
                    make_gates()
                if has_c:
                    dve.wait_ge(pe_y, c + 1)
                    if c >= 2:
                        dve.wait_ge(rows_out, 16 * (c - 1))
                        dve.wait_ge(pool_oh, c - 1)
                    if has_b:
                        v.tensor_tensor(rows[hc][:, :, 0, :], ps[:, 7, :].rearrange("p (t e) -> p t e", e=E),
                                        x_all[:, c * HALF:(c + 1) * HALF, :], ALU.add).then_inc(dve_x1, 1)
                    else:
                        for n in range(2):
                            dve.wait_ge(pe_y, c + 1 + n)
                            v.tensor_tensor(rows[hc][:, 2 * n:2 * n + 2, 0, :],
                                            ps[:, 3 - 2 * n, 0:2 * E].rearrange("p (t e) -> p t e", e=E),
                                            x_all[:, c * HALF + 2 * n:c * HALF + 2 * n + 2, :], ALU.add)
                    order()
                    statistics([rows[hc][:, j, 0, :] for j in range(HALF)], stats2, mean_var2)
                if has_b:
                    mask_attention(u, 1)
                if has_c and not late:
                    root_seed(mean_var2[:, :, :], rstd2[:, :], var[:, 0:HALF])
                    root_steps(rstd2[:, :], var[:, 0:HALF], 1)
                if has_b:
                    mask_sums(u, 1)
                    order()
                if has_c and not late:
                    root_steps(rstd2[:, :], var[:, 0:HALF], 2)
                if has_b:
                    mask_attention(u, 2)
                if late:
                    root_seed(mean_var2[:, :, :], rstd2[:, :], var[:, 0:HALF])
                    root_steps(rstd2[:, :], var[:, 0:HALF], 1)
                if has_a:
                    dve.wait_ge(act_eq, s + 1)
                    v.scalar_tensor_tensor(q_t[h][:, :], e_q[h][:, :], 1.0, q_t[h][:, :], ALU.min,
                                           ALU.add).then_inc(dve_q, 1)
                    dve.wait_ge(act_ek, s + 1)
                    v.scalar_tensor_tensor(k_t[h][:, :], e_k[h][:, :], 1.0, k_t[h][:, :], ALU.min,
                                           ALU.add).then_inc(dve_k, 1)
                if has_c and not late:
                    scale_x1(c)
                if has_b:
                    mask_sums(u, 2)
                if has_b:
                    mask_attention(u, 3)
                if has_c and not late:
                    if not has_b:
                        order()
                    make_h2(c)
                if late:
                    root_steps(rstd2[:, :], var[:, 0:HALF], 2)
                if has_a:
                    dve.wait_ge(act_qhi, s + 1)
                    v.scalar_tensor_tensor(q_lo[h][:, :], q_t[h][:, :], SPREAD, q_hi[h][:, :], ALU.mult,
                                           ALU.subtract).then_inc(dve_qlo, 1)
                    dve.wait_ge(act_khi, s + 1)
                    v.scalar_tensor_tensor(k_lo[h][:, :], k_t[h][:, :], SPREAD, k_hi[h][:, :], ALU.mult,
                                           ALU.subtract).then_inc(dve_klo, 1)
                if has_b:
                    mask_sums(u, 3)
                if has_a:
                    for k in range(HG):
                        last = v.tensor_scalar(kx_hi[h][:, :, k, :], k_hi[h][:, :].rearrange("p (c m) -> p c m", m=CHUNK),
                                               head_mask[:, k:k + 1], None, ALU.mult)
                    if s == 0:
                        order()
                        for k in range(HG):
                            last = v.tensor_scalar(kx_lo[h][:, :, k, :],
                                                   k_lo[h][:, :].rearrange("p (c m) -> p c m", m=CHUNK),
                                                   head_mask[:, k:k + 1], None, ALU.mult)
                    last.then_inc(dve_kx, 1)
                if u < 0:
                    root_seed(mean_var[:, HALF:, :], rstd[:, HALF:], var[:, HALF:])
                    root_steps(rstd[:, HALF:], var[:, HALF:], 3)
                    v.memset(den[0][:, :], 0.0).then_inc(dve_stats, 1)
                if u == 3:
                    dve.wait_ge(pe_perm, 1)
                    v.tensor_tensor(table[:, :], table[:, :], ps[:, 7, 0:P], ALU.add).then_inc(dve_perm, 1)
                if late:
                    scale_x1(c)
                if has_b:
                    divide(u, 0)
                if late:
                    make_h2(c)
                if has_b:
                    divide(u, 1)
                if has_a:
                    for n in range(2):
                        two_tiles = slice(2 * n, 2 * n + 2)
                        dve.wait_ge(act_vt, 2 * s + n + 1)
                        v.scalar_tensor_tensor(k_tok[h][:, two_tiles, :], e_kt[h][:, two_tiles, :], 1.0,
                                               k_tok[h][:, two_tiles, :], ALU.min, ALU.add).then_inc(dve_kt, 1)
                if has_b:
                    divide(u, 2)
                    divide(u, 3)

            c0 = (STEPS - 2) * HALF
            whole = rt_g[:, c0:]
            order()
            v.tensor_tensor(rt_s[1][:, :].rearrange("p (k t) -> p k t", k=2), rows_all[:, :, :, 1, 0],
                            rows_all[:, :, :, 1, 1], ALU.add)
            order()
            v.scalar_tensor_tensor(rt_t[1][:, :], rt_s[1][:, :], -1.0, rt_s[1][:, :], ALU.mult, ALU.max)
            v.scalar_tensor_tensor(rt_i[1][:, :], rt_s[1][:, :], -1.0, rt_s[1][:, :], ALU.mult, ALU.max)
            v.tensor_scalar(whole, rt_s[1][:, :], 0.0, 2.0, ALU.is_ge, ALU.mult)
            order()
            v.tensor_copy(rt_f[1][:, :], rt_i[1][:, :])
            order()
            v.tensor_tensor(rt_m[1][:, :], rt_f[1][:, :], rt_t[1][:, :], ALU.is_gt)
            order()
            v.tensor_tensor(rt_f[1][:, :], rt_f[1][:, :], rt_m[1][:, :], ALU.subtract)
            order()
            v.scalar_tensor_tensor(rt_i[1][:, :], whole, -1.0, rt_f[1][:, :], ALU.add, ALU.mult)
            order()
            v.tensor_scalar(rt_i2[:, :], rt_i[1][:, :], EXPERTS - 1, None, ALU.bitwise_and)
            order()
            v.tensor_copy(whole, rt_i2[:, :])
            order()
            v.tensor_tensor(onehot[:, c0:, :], iota_row[:, 0:EXPERTS].unsqueeze(1).broadcast_to([P, 2 * HALF, EXPERTS]),
                            whole.unsqueeze(2).broadcast_to([P, 2 * HALF, EXPERTS]), ALU.is_equal).then_inc(dve_oh, 1)
            dve.wait_ge(pe_perm, STEPS - 2)
            v.tensor_tensor(table[:, :], table[:, :], ps[:, 7, 0:P], ALU.add).then_inc(dve_perm, 1)

            all_s = [P, SLOTS, EXPERTS]
            dve.wait_ge(pe_total, 1)
            v.tensor_scalar(tot_i[:, :], ps[:, 5, 0:EXPERTS], float(P - 1), None, ALU.add)
            v.tensor_tensor(rank8[1][:, :, :], ps[:, 6, 0:2 * HALF * EXPERTS].rearrange("p (t e) -> p t e", e=EXPERTS),
                            onehot[:, c0:, :], ALU.mult)
            order()
            v.tensor_scalar(tot_i[:, :], tot_i[:, :], 7, None, ALU.logical_shift_right)
            v.tensor_reduce(rt_r[1][:, :], rank8[1][:, :, :], axis=AX.X, op=ALU.add)
            order()
            v.tensor_copy(tiles_of[:, :], tot_i[:, :])
            v.tensor_copy(rt_i[1][:, :], rt_r[1][:, :])
            order()
            v.tensor_copy(ends[0][:, 0:1], tiles_of[:, 0:1])
            v.tensor_tensor(ends[0][:, 1:], tiles_of[:, 1:], tiles_of[:, 0:EXPERTS - 1], ALU.add)
            v.tensor_scalar(rt_i2[:, :], rt_i[1][:, :], P - 1, None, ALU.bitwise_and)
            v.tensor_scalar(rt_i3[:, :], rt_i[1][:, :], 7, None, ALU.logical_shift_right)
            order()
            v.tensor_copy(ends[1][:, 0:2], ends[0][:, 0:2])
            v.tensor_tensor(ends[1][:, 2:], ends[0][:, 2:], ends[0][:, 0:EXPERTS - 2], ALU.add)
            v.tensor_copy(rt_r[1][:, :], rt_i2[:, :])
            v.tensor_copy(rt_k[1][:, :], rt_i3[:, :])
            order()
            v.tensor_copy(ends[0][:, 0:4], ends[1][:, 0:4])
            v.tensor_tensor(ends[0][:, 4:], ends[1][:, 4:], ends[1][:, 0:EXPERTS - 4], ALU.add)
            v.scalar_tensor_tensor(rt_k[1][:, :], whole, float(PLACES), rt_k[1][:, :], ALU.mult, ALU.add)
            order()
            v.tensor_tensor(passed, ends[0][:, :].unsqueeze(1).broadcast_to(all_s),
                            iota_row[:, 0:SLOTS].unsqueeze(2).broadcast_to(all_s), ALU.is_le).then_inc(dve_passed, 1)
            v.tensor_tensor(oh_place[1][:, :, :], iota_row[:, :].unsqueeze(1).broadcast_to([P, 2 * HALF, P]),
                            rt_r[1][:, :].unsqueeze(2).broadcast_to([P, 2 * HALF, P]), ALU.is_equal)
            for j in range(2 * HALF):
                t = c0 + j
                last = v.tensor_scalar(oh_token[1][:, j, :], iota_row[:, :], rt_k[1][:, j:j + 1],
                                       token1[:, t:t + 1], ALU.is_equal, ALU.mult)
                if j % HALF == HALF - 1:
                    last.then_inc(dve_v, 1)
            dve.wait_ge(pool_slots, 1)
            v.tensor_tensor(slot_c[:, :], iota_row[:, 0:SLOTS], slot_b, ALU.subtract)
            order()
            v.scalar_tensor_tensor(slot_c[:, :], slot_g, float(PLACES), slot_c[:, :], ALU.mult, ALU.add)
            dve.wait_ge(pe_perm, STEPS - 1)
            v.tensor_tensor(table16[:, :], table[:, :], ps[:, 4, 0:P], ALU.add)
            order()
            v.tensor_scalar(pick[:, :], slot_c[:, :], part_f[:, 0:1], None, ALU.is_equal).then_inc(dve_pick, 1)
            v.tensor_copy(slot_gi[:, :], slot_g)
            order()
            v.tensor_scalar(slot_gm[:, :], slot_gi[:, :], EXPERTS - 1, None, ALU.bitwise_and)
            dve.wait_ge(pe_slots, 1)
            v.tensor_copy(tok_f[:, :], ps[:, 2, 0:SLOTS])
            order()
            v.tensor_scalar(src_f[:, :], tok_f[:, :], -1.0, 0.0, ALU.add, ALU.max)
            order()
            v.tensor_copy(src_i[:, :], src_f[:, :]).then_inc(dve_src, 1)
            v.tensor_scalar(tok_e[:, :], tok_f[:, :], 0.5, part_far[:, 0:1], ALU.is_lt, ALU.mult)
            v.tensor_scalar(second[:, :], tok_f[:, :], L + 0.5, None, ALU.is_gt)
            v.tensor_scalar(first[:, :], tok_f[:, :], L + 0.5, None, ALU.is_lt)
            order()
            v.tensor_tensor(dst_f[:, :], tok_e[:, :], src_f[:, :], ALU.add)
            order()
            v.tensor_copy(dst_i[:, :], dst_f[:, :]).then_inc(dve_slots, 1)
            order()

            v.memset(den[0][:, :], 0.0).then_inc(y_free, 2)

            def stage_w1(n, k):
                expert = dve.value_load(slot_gm[0:1, bass.ds(n, 1)], min_val=0, max_val=EXPERTS - 1)
                v.tensor_copy(w1_now[k][:, :, :, :], w1_parts[:, bass.ds(expert, 2), :, :]).then_inc(dve_w1, 1)

            def low_part(n, k):
                dve.wait_ge(act_hT, n + 1)
                v.scalar_tensor_tensor(h_lo[k][:, :], ps[:, 6 + k, 0:P], SPREAD, h_hi[k][:, :], ALU.mult,
                                       ALU.subtract).then_inc(dve_hlo, 1)

            def relu_second(n):
                dve.wait_ge(act_bias, n + 1)
                dve.wait_ge(pe_w1, n * 2 + 2)
                for c in range(FC):
                    last = v.tensor_scalar(hid[1][:, 1, c, :], ps[:, 3, c * P:(c + 1) * P],
                                           b1_now[:, bass.ds(n, 1), FC + c], 0.0, ALU.add, ALU.max)
                last.then_inc(dve_hid, 1)

            def finish(n, k):
                dve.wait_ge(act_gate, n + 1)
                v.scalar_tensor_tensor(gate_b[k][:, :], gates[:, 0, 1, :], first[:, bass.ds(n, 1)], gate_a[k][:, :],
                                       ALU.mult, ALU.add)
                dve.wait_ge(pe_y2, n + 1)
                v.scalar_tensor_tensor(y_b[k][:, :], ps[:, 4 + k, 0:E], 1.0 / SPREAD ** 2,
                                       b2_now[:, bass.ds(n, 1), :].rearrange("p a e -> p (a e)"),
                                       ALU.mult, ALU.add).then_inc(y_free, 1)
                order()
                dve.wait_ge(gated_free, n + 1)
                v.tensor_tensor(y_g[k][:, :], y_b[k][:, :], gate_b[k][:, :], ALU.mult).then_inc(dve_gated, 1)

            def row(n, k, pair):
                wait_alone(dve, gathered[k], pair * 16 + 16)
                v.tensor_copy(h_row[k][:, :], got[:, bass.ds(n, 1), 1, :].rearrange("p a e -> p (a e)")
                              ).then_inc(dve_row, 1)

            def slot(n, k, next_pair):
                dve.wait_ge(pe_w1, n * 2 + 2)
                stage_w1(n + 2, k)
                low_part(n + 2, k)
                if next_pair is not None:
                    wait_alone(dve, pe_hT, n + 2)
                    row(n + 3, 1 - k, next_pair)
                if k == 0:
                    relu_second(n + 1)
                finish(n, k)

            dve.wait_ge(pool_w1lo, 1)
            dve.wait_ge(pe_y, STEPS + 1)
            for n in range(2):
                stage_w1(n, n)
            for n in range(2):
                row(n, n, 0)
            low_part(0, 0)
            dve.wait_ge(pe_hT, 1)
            row(2, 0, 1)
            low_part(1, 1)
            unrolled = 4
            full_turns = (SLOTS - 2) // unrolled
            with dve.Fori(0, full_turns) as i:
                for m in range(unrolled):
                    slot(i * unrolled + m, m % 2, i * (unrolled // 2) + (m + 3) // 2)
            for n in range(full_turns * unrolled, SLOTS):
                k = n % 2
                if n + 2 < SLOTS:
                    slot(n, k, (n + 3) // 2 if n + 3 < SLOTS else None)
                else:
                    if k == 0 and n + 1 < SLOTS:
                        relu_second(n + 1)
                    finish(n, k)

        @block.tensor
        def _(pe):
            def mm(out, lhsT, rhs, start=True, stop=True, **k):
                return nc.tensor.matmul(out, lhsT, rhs, start=start, stop=stop, **k)

            def tr(out, src, n=P):
                return nc.tensor.transpose(out, src, ident[0:n, 0:n])

            def warm(n):
                for _ in range(n):
                    mm(ps[:, 0, :], ones[:, :], ones[:, :].unsqueeze(1).broadcast_to([P, 512 // P, P]))

            pe.wait_ge(const, 1)
            pe.wait_ge(in_small, 80)
            tr(ps[:, 0, 0:B], c_rows[0:B, :], B)
            for k in range(3):
                tr(ps[:, 1, k * P:(k + 1) * P], wqkv[:, k, :])
            tr(ps[:, 2, 0:P], wout[:, :])
            tr(ps[:, 3, 0:EXPERTS * FC], b1_rows[0:EXPERTS * FC, :], EXPERTS * FC).then_inc(setup_pe, 1)
            def chunk_attention(s, r):
                h, i = s % 2, GROUPS * s + r
                if r == 0:
                    pe.wait_ge(dve_qlo, s + 1)
                    pe.wait_ge(dve_kx, s + 1)
                    if s:
                        pe.wait_ge(act_kx, s)
                if i >= 2:
                    pe.wait_ge(dve_at, i - 1)
                rp = slice(r * CHUNK, (r + 1) * CHUNK)
                for c in range(CPH):
                    o = ps[:, r % 2, c * CHUNK:(c + 1) * CHUNK]
                    cs = slice(c * CHUNK, (c + 1) * CHUNK)
                    hi = kx_hi[h][rp, c, :, :].rearrange("p k m -> p (k m)")
                    lo = kx_lo[h][rp, c, :, :].rearrange("p k m -> p (k m)")
                    mm(o, hi, q_hi[h][rp, cs], stop=False)
                    mm(o, hi, q_lo[h][rp, cs], start=False, stop=False)
                    last = mm(o, lo, q_hi[h][rp, cs], start=False)
                last.then_inc(pe_qk, 1)

            def chunk_sums(s, j):
                h = s % 2
                if j == 0:
                    pe.wait_ge(dve_kt, 2 * s + 2)
                if HALF * s + j:
                    pe.wait_ge(dve_sm, HALF * s + j)
                for c in range(CPT):
                    n = (c + 1) * CHUNK
                    last = mm(ps[:, 4 + c // 2, (c % 2) * OW:(c % 2 + 1) * OW], k_tok[h][0:n, j, :],
                              v_tok[h][0:n, j, :, :].rearrange("p g c -> p (g c)"))
                last.then_inc(pe_ds, 1)

            def outputs(s, j):
                h, bank = s % 2, 6 + j % 2
                if j == 0:
                    pe.wait_ge(act_vx, CPT * (s + 1))
                    pe.wait_ge(dve_at, GROUPS * (s + 1))
                pe.wait_ge(dve_st, HALF * s + j + 1)
                if j >= 2:
                    pe.wait_ge(dve_ao, HALF * s + j - 1)
                elif j == 0:
                    if s == 0:
                        pe.wait_ge(dve_gates, 1)
                    elif s >= 2:
                        pe.wait_ge(act_rank, s - 1)
                    else:
                        pe.wait_ge(act_aT, s)
                elif s >= 3:
                    pe.wait_ge(dve_perm, s - 2)
                elif s:
                    pe.wait_ge(dve_x1, s)
                at_start = state[h][:, j, :] if (j or s % HALVES == 0) else state[1 - h][:, HALF, :]
                mm(ps[:, bank, 0:OW], q_t[h][:, j * P:(j + 1) * P], at_start, stop=False, skip_group_check=True)
                for c in range(1, CPT):
                    t = j * P + c * CHUNK
                    mm(ps[c * CHUNK:(c + 1) * CHUNK, bank, 0:OW], q_t[h][:, t:t + CHUNK],
                       part[h][:, j, c - 1, :], start=False, stop=False, skip_group_check=True)
                for c in range(CPT):
                    for r in range(GROUPS):
                        last = mm(ps[c * CHUNK:(c + 1) * CHUNK, bank, r * GW:(r + 1) * GW],
                                  attn[h][:, r, j * CPT + c, :], vx[h][:, j * CPT + c, r, :],
                                  start=False, stop=True, skip_group_check=True)
                last.then_inc(pe_o, 1)

            def ranks(bank, first, n, c):
                out = ps[:, bank, 0:n * EXPERTS].rearrange("p (t e) -> p t e", e=EXPERTS)
                mm(out, before[:, :], onehot[:, first:first + n, :], stop=False, skip_group_check=True)
                for j in range(n - 1):
                    mm(out[:, j + 1:, :], ones[:, :],
                       onehot[:, first + j:first + j + 1, :].broadcast_to([P, n - 1 - j, EXPERTS]),
                       start=False, skip_group_check=True)
                mm(out, ones[:, :], earlier[:, c:c + 1, :].broadcast_to([P, n, EXPERTS]),
                   start=False, skip_group_check=True).then_inc(pe_rank, 1)

            def places(bank, k, n, ready=None):
                for j in range(n):
                    if ready is not None and j % HALF == 0:
                        pe.wait_ge(ready, j // HALF + 1)
                    last = mm(ps[:, bank, 0:P], oh_token[k][:, j, :], oh_place[k][:, j, :], start=(j == 0),
                              stop=(j == n - 1))
                last.then_inc(pe_perm, 1)

            def outputs_transposed(s, j):
                pe.wait_ge(dve_ao, HALF * s + j + 1)
                t = tr(ps[:, 2 - 2 * (j // 2), (j % 2) * P:(j % 2 + 1) * P], heads_out[s % 2][:, j, :])
                if j % 2:
                    t.then_inc(pe_aT, 1)

            def spread(s, f):
                if s == 0 and f < 2:
                    pe.wait_ge(act_vTx, 1)
                elif f < 2:
                    pe.wait_ge(act_vt, 2 * s + f + 1)
                else:
                    pe.wait_ge(act_vx, s * CPT + f - 1)
                for i in range(4):
                    last = tr(ps[:, 2 + f % 2, i * P:(i + 1) * P], vx_t[s % 2][:, 4 * f + i, :, :].rearrange("p k m -> p (k m)"))
                last.then_inc(pe_vx, 1)

            def by_token(s, n):
                for t in range(2):
                    j = 2 * n + t
                    last = mm(ps[:, banks_of(s)[3 + n], t * 256:t * 256 + 256], h_t[s % 2][:, j * P:(j + 1) * P], w_t[:, E:])
                last.then_inc(pe_kv, 1)

            for u in TURNS:
                has_a, has_b, has_c = parts_of(u)
                s, h = u + 1, (u + 1) % 2
                c = u - 1
                if u == 0:
                    pe.wait_ge(act_vt, 2)
                if has_b:
                    chunk_attention(u, 0)
                if u == 0:
                    spread(0, 2)
                    spread(0, 3)
                if has_c and has_b:
                    pe.wait_ge(dve_ao, HALF * (c + 1))
                    for j in range(HALF):
                        last = tr(ps[:, 6, j * P:(j + 1) * P], heads_out[c % 2][:, j, :])
                    last.then_inc(pe_aT, 1)
                if has_b:
                    chunk_sums(u, 0)
                if has_c:
                    for j in range(HALF):
                        if has_b:
                            bank, place, count = 7, j, 1
                        else:
                            bank, place, count = 3 - 2 * (j // 2), j % 2, 1 + j // 2
                        pe.wait_ge(act_aT, c + count)
                        last = mm(ps[:, bank, place * P:(place + 1) * P], a_t[0][:, j * P:(j + 1) * P],
                                  wo_g[:, c // HALVES, :])
                        if j == HALF - 1 or not has_b and j == 1:
                            last.then_inc(pe_y, 1)
                if u < 0:
                    pe.wait_ge(setup_dve, 1)
                    for k in range(2):
                        last = mm(ps[:, 4, k * B:(k + 1) * B], wmod[:, k * E:(k + 1) * E], silu[:, :])
                    last.then_inc(setup_pe, 1)
                if has_a:
                    if s == 0:
                        pe.wait_ge(setup_act, 2)
                        pe.wait_ge(dve_xn, 1)
                    else:
                        pe.wait_ge(pool_xn, s)
                        pe.wait_ge(act_vx, CPT * s - 1)
                    for j in range(HALF):
                        last = tr(ps[:, 2, j * P:(j + 1) * P], xn[h][:, j, :])
                    last.then_inc(pe_xT, 1)
                if has_b:
                    chunk_attention(u, 1)
                if has_a:
                    pe.wait_ge(act_h, s + 1)
                    if s:
                        pe.wait_ge(act_vx, CPT * s)
                    mm(ps[:, 3, :], w_t[:, 0:E], h_t[h][:, :]).then_inc(pe_q, 1)
                if has_b:
                    chunk_sums(u, 1)
                if has_a:
                    mm(ps[:, 2, :], w_t[:, E:2 * E], h_t[h][:, :]).then_inc(pe_k, 1)
                if has_b:
                    chunk_attention(u, 2)
                if has_a:
                    if s:
                        pe.wait_ge(act_eq, s + 1)
                    mm(ps[:, banks_of(s)[2], :], w_t[:, 2 * E:], h_t[h][:, :]).then_inc(pe_vT, 1)
                if has_b:
                    chunk_sums(u, 2)
                if has_a:
                    if s:
                        pe.wait_ge(act_ek, s + 1)
                    by_token(s, 0)
                if has_b:
                    chunk_attention(u, 3)
                if has_a:
                    if s:
                        pe.wait_ge(act_vTx, s + 1)
                    by_token(s, 1)
                if u < 0:
                    pe.wait_ge(setup_dve, 2)
                    for b in range(B):
                        last = mm(ps[:, 6 + b, :], silu_bc[:, b, :], wmod[:, 2 * E:])
                    last.then_inc(setup_pe, 1)
                if has_b:
                    chunk_sums(u, 3)
                if u == 3:
                    pe.wait_ge(pool_v, 1)
                    pe.wait_ge(dve_x1, u)
                    places(7, 0, HALF)
                if u >= 2 and u - 2 < STEPS - 2:
                    pe.wait_ge(pool_oh, u - 1)
                    ranks(6, (u - 2) * HALF, HALF, u - 2)
                if has_a:
                    spread(s, 0)
                    spread(s, 1)
                if has_b:
                    for j in range(HALF):
                        outputs(u, j)
                        if has_a and j < 2:
                            spread(s, 2 + j)
                        if u == STEPS - 1 and j >= 1:
                            outputs_transposed(u, j - 1)
                if u == STEPS - 1:
                    outputs_transposed(u, HALF - 1)

            pe.wait_ge(pool_v, 2)
            places(7, 0, HALF)
            pe.wait_ge(dve_oh, 1)
            ranks(6, (STEPS - 2) * HALF, 2 * HALF, STEPS - 2)
            mm(ps[:, 5, 0:EXPERTS], ones[:, :], earlier[:, STEPS - 2, :], stop=False)
            for t in range((STEPS - 2) * HALF, TILES):
                last = mm(ps[:, 5, 0:EXPERTS], ones[:, :], onehot[:, t, :], start=False, stop=(t == TILES - 1))
            last.then_inc(pe_total, 1)
            warm(12)
            places(4, 1, 2 * HALF, dve_v)
            pe.wait_ge(dve_pick, 1)
            mm(ps[:, 2, 0:SLOTS], table16[:, :], pick[:, :]).then_inc(pe_slots, 1)

            def row_transposed(k):
                tr(ps[:, 6 + k, 0:P], h_row[k][:, :]).then_inc(pe_hT, 1)

            def hidden(k):
                for x in range(2):
                    for c in range(FC):
                        o, cs = ps[:, 2 * k + x, c * P:(c + 1) * P], slice(c * P, (c + 1) * P)
                        mm(o, w1_now[k][:, x, 0, cs], h_hi[k][:, :], stop=False)
                        mm(o, w1_now[k][:, x, 0, cs], h_lo[k][:, :], start=False, stop=False)
                        last = mm(o, w1_now[k][:, x, 1, cs], h_hi[k][:, :], start=False)
                    last.then_inc(pe_w1, 1)

            def second_layer(k, x, expert):
                for c in range(FC):
                    last = mm(ps[:, 4 + k, 0:E], hid[k][:, x, c, :],
                              w2[:, bass.ds(expert + x, 1), c, :].rearrange("p a e -> p (a e)"),
                              start=(x == 0 and c == 0), stop=(x == 1 and c == FC - 1))
                return last

            warm(11)
            pe.wait_ge(in_w2, 16 * (EXPERTS + 1))
            pe.wait_ge(dve_slots, 1)
            for k in range(2):
                pe.wait_ge(dve_row, k + 1)
                row_transposed(k)
            pe.wait_ge(dve_w1, 1)
            pe.wait_ge(dve_hlo, 1)
            hidden(0)

            def slot(n, k, pair):
                expert = pe.value_load(slot_gm[0:1, bass.ds(n, 1)], min_val=0, max_val=EXPERTS - 1)
                pe.wait_ge(dve_row, n + 3)
                row_transposed(k)
                pe.wait_ge(dve_w1, n + 2)
                pe.wait_ge(dve_hlo, n + 2)
                hidden(1 - k)
                pe.wait_ge(y_free, n + 1)
                pe.wait_ge(act_hid, n + 1)
                second_layer(k, 0, expert)
                pe.wait_ge(dve_hid if k else act_hid2, pair + 1)
                second_layer(k, 1, expert).then_inc(pe_y2, 1)

            with pe.Fori(0, SLOTS // 2 - 1) as i:
                slot(i * 2, 0, i)
                slot(i * 2 + 1, 1, i)
            for n in range(SLOTS - SLOTS % 2 - 2, SLOTS):
                k = n % 2
                expert = pe.value_load(slot_gm[0:1, n:n + 1], min_val=0, max_val=EXPERTS - 1)
                if n + 2 < SLOTS:
                    pe.wait_ge(dve_row, n + 3)
                    row_transposed(k)
                if n + 1 < SLOTS:
                    pe.wait_ge(dve_w1, n + 2)
                    pe.wait_ge(dve_hlo, n + 2)
                    hidden(1 - k)
                pe.wait_ge(y_free, n + 1)
                pe.wait_ge(act_hid, n + 1)
                second_layer(k, 0, expert)
                pe.wait_ge(dve_hid if k else act_hid2, n // 2 + 1)
                second_layer(k, 1, expert).then_inc(pe_y2, 1)


_INS = ["L0_attn_x", "L0_attn_W_qkv", "L0_attn_W_out", "L0_ffn_W1", "L0_ffn_b1", "L0_ffn_W2", "L0_ffn_b2",
        "L0_c", "L0_wmod"]


def kernel(**inputs):
    import numpy as np
    import concourse.bacc as bacc
    from concourse.bass_utils import run_bass_kernel_spmd

    nc = bacc.Bacc("TRN2", target_bir_lowering=False, num_devices=1)
    arrays, aps = {}, []
    for name in _INS:
        a = np.ascontiguousarray(inputs[name])
        if name == "L0_attn_x":
            a = a.reshape(B * L, E)
        arrays[f"in_{name}"] = a
        aps.append(nc.dram_tensor(f"in_{name}", a.shape, mybir.dt.from_np(a.dtype), kind="ExternalInput").ap())
    out = nc.dram_tensor("out_rows", (B * L, E), F32, kind="ExternalOutput").ap()
    build(nc, *aps, out)
    r = run_bass_kernel_spmd(nc, [arrays], core_ids=[0])
    return r.results[0]["out_rows"].reshape(B, L, E)
```
